# Optimizing a Trainium2 kernel written in Bass

```python
import numpy as np
import jax
import jax.numpy as jnp

def _softmax(x, axis=-1):
    return jax.nn.softmax(x, axis=axis)

def _gelu(x):
    return jax.nn.gelu(x, approximate=True)

def _silu(x):
    return jax.nn.silu(x)

def _sigmoid(x):
    return jax.nn.sigmoid(x)

def _layernorm(x, axis=-1, eps=1e-05):
    m = jnp.mean(x, axis=axis, keepdims=True)
    v = jnp.var(x, axis=axis, keepdims=True)
    return (x - m) / jnp.sqrt(v + eps)

def _scatter_add(tgt, idx, src, axis=0):
    return tgt.at[idx].add(src)

def _segment_sum(src, seg, n):
    return jax.ops.segment_sum(src, seg, n)
kernel_name = 'mk_gnn_resnorm_d1_gnn_r32_c59dbb'

def setup_inputs(seed: int=0):
    np.random.seed(seed)
    _w = jnp.asarray

    def _rec_inputs():
        import jax
        import jax.numpy as jnp
        _gk = jax.random.key(seed)
        x = -0.0003713 + 1 * jax.random.normal(jax.random.fold_in(_gk, 1), (3125, 256), jnp.float32)
        src = jax.random.randint(jax.random.fold_in(_gk, 2), (50000,), 0, 3125, jnp.int32)
        dst = jax.random.randint(jax.random.fold_in(_gk, 3), (50000,), 0, 3125, jnp.int32)
        _o = jnp.argsort(dst, stable=True)
        src = src[_o]
        dst = dst[_o]
        edge_type_8 = jax.random.randint(jax.random.fold_in(_gk, 12), (50000,), 0, 8, jnp.int32)
        return (x, src, dst, edge_type_8)
    x, src, dst, edge_type_8 = _rec_inputs()

    def _L0_gnn_setup():
        import jax, jax.numpy as jnp
        import numpy as np
        N, E = (50000, 25000)
        IN = HID = OUT = 256
        K = 3

        def _gcn_norm(edge_index, num_nodes):
            row, col = (edge_index[0], edge_index[1])
            deg = jax.ops.segment_sum(jnp.ones((edge_index.shape[1],), jnp.float32), col, num_segments=num_nodes)
            dis = jnp.where(deg > 0, jax.lax.rsqrt(jnp.maximum(deg, 1.0)), 0.0)
            return dis[row] * dis[col]

        def _tagconv(x, src, dst, norm, W, b):
            out = x @ W[0]
            h = x
            for k in range(1, K + 1):
                msg = norm[:, None] * h[src]
                h = jax.ops.segment_sum(msg, dst, num_segments=x.shape[0])
                out = out + h @ W[k]
            return out + b
        key = jax.random.key(seed)
        ks = jax.random.split(key, 9)
        s = 0.02
        return {'x': jax.random.normal(ks[0], (N, IN), dtype=jnp.float32), 'edge_index': jax.random.randint(ks[1], (2, E), 0, N, dtype=jnp.int32), 'edge_type': jax.random.randint(ks[2], (E,), 0, 8, dtype=jnp.int32), 'W1': jax.random.normal(ks[3], (K + 1, IN, HID), dtype=jnp.float32) * s, 'b1': jnp.zeros((HID,), dtype=jnp.float32), 'W2': jax.random.normal(ks[4], (K + 1, HID, HID), dtype=jnp.float32) * s, 'b2': jnp.zeros((HID,), dtype=jnp.float32), 'W3': jax.random.normal(ks[5], (K + 1, HID, OUT), dtype=jnp.float32) * s, 'b3': jnp.zeros((OUT,), dtype=jnp.float32)}
    _L0_gnn_all = _L0_gnn_setup()
    _L0_gnn_in = {k: v for k, v in _L0_gnn_all.items() if k in ('W1', 'b1', 'W2', 'b2', 'W3', 'b3')}
    del _L0_gnn_all
    return {'x': x, 'src': src, 'dst': dst, 'edge_type_8': edge_type_8, 'L0_gnn_W1': _L0_gnn_in['W1'], 'L0_gnn_b1': _L0_gnn_in['b1'], 'L0_gnn_W2': _L0_gnn_in['W2'], 'L0_gnn_b2': _L0_gnn_in['b2'], 'L0_gnn_W3': _L0_gnn_in['W3'], 'L0_gnn_b3': _L0_gnn_in['b3']}

def reference(x, src, dst, edge_type_8, L0_gnn_W1, L0_gnn_b1, L0_gnn_W2, L0_gnn_b2, L0_gnn_W3, L0_gnn_b3):
    import jax
    import jax.numpy as jnp

    def _L0_gnn_ref(x, edge_index, edge_type, W1, b1, W2, b2, W3, b3):
        import jax, jax.numpy as jnp
        import numpy as np
        N, E = (50000, 25000)
        IN = HID = OUT = 256
        K = 3

        def _gcn_norm(edge_index, num_nodes):
            row, col = (edge_index[0], edge_index[1])
            deg = jax.ops.segment_sum(jnp.ones((edge_index.shape[1],), jnp.float32), col, num_segments=num_nodes)
            dis = jnp.where(deg > 0, jax.lax.rsqrt(jnp.maximum(deg, 1.0)), 0.0)
            return dis[row] * dis[col]

        def _tagconv(x, src, dst, norm, W, b):
            out = x @ W[0]
            h = x
            for k in range(1, K + 1):
                msg = norm[:, None] * h[src]
                h = jax.ops.segment_sum(msg, dst, num_segments=x.shape[0])
                out = out + h @ W[k]
            return out + b
        src, dst = (edge_index[0], edge_index[1])
        norm = _gcn_norm(edge_index, x.shape[0])
        h = jax.nn.relu(_tagconv(x, src, dst, norm, W1, b1))
        h = jax.nn.relu(_tagconv(h, src, dst, norm, W2, b2))
        return _tagconv(h, src, dst, norm, W3, b3)
    edge_index = jnp.stack([src, dst])
    x = _layernorm(x + _L0_gnn_ref(x, edge_index, edge_type_8, L0_gnn_W1, L0_gnn_b1, L0_gnn_W2, L0_gnn_b2, L0_gnn_W3, L0_gnn_b3), axis=-1)
    return x

_drawn_inputs = setup_inputs


def setup_inputs(seed=0):
    import zlib

    import numpy as np

    out = dict(_drawn_inputs(seed))
    spreads = {'L0_gnn_b1': (0.0, 0.544), 'L0_gnn_b2': (0.0, 0.1), 'L0_gnn_b3': (0.0, 0.1)}
    factors = {'L0_gnn_W1': 3.608}
    for name, (base, spread) in spreads.items():
        noise = np.random.default_rng([zlib.crc32(name.encode()), seed]).standard_normal(out[name].shape)
        drawn = base * np.exp(spread * noise) if base else spread * noise
        out[name] = jnp.asarray(drawn.astype(out[name].dtype))
    for name, factor in factors.items():
        out[name] = (out[name] * factor).astype(out[name].dtype)
    return out
```

```python
from contextlib import ExitStack

import concourse.bass as bass
from concourse import mybir

P = 128
N = 3125
E = 50000
F = 256
NT = 25
NP = NT * P
TAIL = N - (NT - 1) * P
GW = 11
NG = 285
BG = 95
NQ = 3
KEYS = NT * GW
WIN = 256
GRAN = 16
NR = 8
SB_ = 6
NB = 4
RB = 4
SC = 2048.0
SV = 16.0
EPS = 1e-5
NCH = -(-E // P)
PT = 9
LOW = 2.0 ** -10
HIGH = 60000.0
AMAX = 87.5
NAM = 125

ALU = mybir.AluOpType
ACT = mybir.ActivationFunctionType
AX = mybir.AxisListType
F32 = mybir.dt.float32
F16 = mybir.dt.float16
F8 = mybir.dt.float8e4
I32 = mybir.dt.int32
I16 = mybir.dt.int16
U8 = mybir.dt.uint8


def rows(t):
    return P if t < NT - 1 else TAIL


def schedule():
    out = [("T", 0, 0), ("T", 0, 1)]
    for t in range(NT):
        if t + 2 < NT:
            out.append(("T", 0, t + 2))
        out.append(("P", 0, 3, t))
    for L in range(3):
        for k in (2, 1, 0):
            for t in range(NT):
                out.append(("P", L, k, t))
                if k == 0 and L < 2:
                    if t >= 1:
                        out.append(("T", L + 1, t - 1))
                    if t >= 2:
                        out.append(("P", L + 1, 3, t - 2))
        if L < 2:
            out.append(("T", L + 1, NT - 1))
            out.append(("P", L + 1, 3, NT - 2))
            out.append(("P", L + 1, 3, NT - 1))
    return out


def general_path(nc, x, edges, Ws, bb, vd, out, A8, bank, cst, dg, w, g, lnb, identf, onesf, S, s_msg):
    line = []
    region = A8[:, :, :].rearrange("p a b -> p (a b)")
    at = [0]

    def take(n, dt=F32):
        v = region[:, at[0]:at[0] + 4 * n].bitcast(dt)
        at[0] += 4 * n
        return v

    gTs = take(2 * NP).rearrange("p (c n) -> p c n", c=2)
    Wf = take(2048).rearrange("p (c k n) -> p c k n", c=2, k=4)
    iot = take(PT * P)
    oh = take(PT * P)
    msg = take(F)
    srcI = take(NCH, I32)
    dstI = take(NCH, I32)
    dstF = take(NCH)
    tmI = take(NCH, I32)
    dhi = take(NCH)
    dlo = take(NCH)
    sm = take(16)
    smi = take(4, I32)

    def op(name, fn, inc=1):
        line.append((name, fn, inc))

    def loop(fns, lp):
        line.append(("loop", fns, lp))

    def opened(e):
        e.sem_inc(S["s_ld"], 1)
        e.sem_inc(S["s_turn"], 1)

    op("sp", opened, 0)
    op("sp", lambda e: e.dma_start(srcI, edges[0, :, :]), 16)
    op("sp", lambda e: e.dma_start(dstI, edges[1, :, :]), 16)
    op("pool", lambda e: e.iota(iot, pattern=[[1, PT * P]], base=0, channel_multiplier=0,
                                allow_small_or_imprecise_dtypes=True))
    op("dve", lambda e: e.tensor_copy(dstF, dstI))
    op("dve", lambda e: e.tensor_scalar(tmI, dstI, 7, None, ALU.logical_shift_right))
    op("dve", lambda e: e.tensor_copy(dhi, tmI))
    op("dve", lambda e: e.tensor_scalar(tmI, dstI, P - 1, None, ALU.bitwise_and))
    op("dve", lambda e: e.tensor_copy(dlo, tmI))
    op("dve", lambda e: e.memset(oh, 0.0))
    DG = bank[7]
    op("pe", lambda e: e.matmul(DG[:, 0:NT], oh[:, 0:P], oh[:, 0:NT], start=True, stop=False, skip_group_check=True))
    loops = [0]

    def deg_dve(e, i, n0):
        e.wait_ge(S["s_ld"], i + n0 + 1)
        e.tensor_scalar(oh[:, 0:P], iot[:, 0:P], dlo[:, bass.ds(i, 1)], None, ALU.is_equal)
        e.tensor_scalar(oh[:, P:P + NT], iot[:, 0:NT], dhi[:, bass.ds(i, 1)], None,
                        ALU.is_equal).then_inc(S["s_lp"], 1)

    def deg_pe(e, i, n0):
        e.wait_ge(S["s_lp"], i + n0 + 1)
        e.matmul(DG[:, 0:NT], oh[:, 0:P], oh[:, P:P + NT], start=False, stop=False,
                 skip_group_check=True).then_inc(S["s_ld"], 1)

    loop({"dve": deg_dve, "pe": deg_pe}, 0)
    op("dve", lambda e: e.tensor_copy(dg[:, 0, :], DG[:, 0:NT]))
    op("dve", lambda e: e.tensor_scalar(dg[:, 1, :], dg[:, 0, :], 1.0, None, ALU.max))
    op("act", lambda e: e.activation(dg[:, 2, :], dg[:, 1, :], ACT.Sqrt))
    op("dve", lambda e: e.reciprocal(dg[:, 3, :], dg[:, 1, :]))
    op("dve", lambda e: e.tensor_scalar(dg[:, 4, :], dg[:, 0, :], 1.0, None, ALU.min))
    op("dve", lambda e: e.tensor_tensor(cst[:, 0, :], dg[:, 3, :], dg[:, 4, :], ALU.mult))
    op("dve", lambda e: e.reciprocal(dg[:, 5, :], dg[:, 2, :]))
    op("dve", lambda e: e.tensor_tensor(dg[:, 6, :], dg[:, 5, :], dg[:, 1, :], ALU.mult))
    op("dve", lambda e: e.tensor_tensor(dg[:, 7, :], dg[:, 6, :], dg[:, 2, :], ALU.add))
    op("dve", lambda e: e.tensor_scalar(cst[:, 2, :], dg[:, 7, :], 0.5, None, ALU.mult))
    op("dve", lambda e: e.reciprocal(cst[:, 3, :], cst[:, 2, :]))
    wt, wu = w[:, 0, :], w[:, 1, :]
    gt, xt = g[:, 0, :], g[:, 1, :]

    def turned(t):
        for c in range(2):
            op("pe", lambda e, c=c: e.transpose(bank[6][:, c * P:(c + 1) * P], gt[:, c * P:(c + 1) * P],
                                                identf[:, :]))
        op("dve", lambda e: e.tensor_copy(gTs[:, :, t * P:(t + 1) * P],
                                          bank[6][:, 0:F].rearrange("p (c m) -> p c m", c=2)))

    def project(L, k, t, acc, first):
        for c in range(2):
            op("pe", lambda e, c=c: e.matmul(acc, gTs[:, c, t * P:(t + 1) * P], Wf[:, c, k, :],
                                             start=(first and c == 0), stop=False, skip_group_check=True))

    def v_out(t, acc, b):
        op("dve", lambda e: e.tensor_scalar(wt, acc, cst[:, 0, t:t + 1], None, ALU.mult))
        op("sp", lambda e: e.dma_start(vd[b][t * P:(t + 1) * P, :], wt), 16)

    op("dve", lambda e: e.memset(xt, 0.0))
    for t in range(NT):
        op("sp", lambda e, t=t: e.dma_start(xt[0:rows(t), :], x[t * P:t * P + rows(t), :]), 16)
        op("dve", lambda e, t=t: e.tensor_scalar(gt, xt, cst[:, 2, t:t + 1], None, ALU.mult))
        turned(t)
    for L in range(3):
        for c in range(2):
            op("sp", lambda e, L=L, c=c: e.dma_start(
                Wf[:, c, :, :], Ws[L][:, c * P:(c + 1) * P, :].rearrange("k f n -> f k n")), 16)
        for t in range(NT):
            acc = bank[0][:, 0:F]
            project(L, 3, t, acc, True)
            v_out(t, acc, 1)
        for k in (2, 1, 0):
            for q in range(NQ):
                tiles = list(range(q * PT, min(NT, (q + 1) * PT)))
                accs = {t: bank[(t - q * PT) // 2][:, F * ((t - q * PT) % 2):F * ((t - q * PT) % 2) + F]
                        for t in tiles}
                for t in tiles:
                    project(L, k, t, accs[t], (t - q * PT) % 2 == 0)
                loops[0] += 1

                def hop_dve(e, i, n0, q=q):
                    e.wait_ge(S["s_ld"], i + n0 + 1)
                    e.tensor_copy(smi[:, 0:1], srcI[:, bass.ds(i, 1)])
                    e.tensor_scalar(sm[:, 0:1], dstF[:, bass.ds(i, 1)], float(-q * PT * P), None,
                                    ALU.add).then_inc(S["s_lp"], 1)
                    e.wait_ge(S["s_lp"], 2 * i + n0 + n0 - NCH + 1)
                    e.tensor_scalar(oh, iot, sm[:, 0:1], None, ALU.is_equal).then_inc(S["s_lp"], 1)

                def hop_pool(e, i, n0, ms=s_msg[loops[0] - 1], src=vd[(k + 1) % 2 if k < 2 else 1]):
                    e.wait_ge(S["s_lp"], 2 * i + n0 + n0 - NCH + 1)
                    e.sem_inc(S["s_pl"], 1)
                    e.indirect_dma_start(msg, None, src[:, :],
                                         bass.IndirectOffsetOnAxis(ap=smi[:, 0:1], axis=0)).then_inc(ms, 16)

                def hop_pe(e, i, n0, ms=s_msg[loops[0] - 1], tiles=tiles, accs=accs):
                    e.wait_ge(S["s_lp"], 2 * i + n0 + n0 - NCH + 2)
                    e.wait_ge(ms, i * 16 + 16)
                    for n, t in enumerate(tiles):
                        mm = e.matmul(accs[t], oh[:, n * P:(n + 1) * P], msg, start=False, stop=False,
                                      skip_group_check=True)
                    mm.then_inc(S["s_ld"], 1)

                loop({"dve": hop_dve, "pool": hop_pool, "pe": hop_pe}, loops[0])
                for t in tiles:
                    acc = accs[t]
                    if k > 0:
                        v_out(t, acc, k % 2)
                        continue
                    if L < 2:
                        op("dve", lambda e, L=L, t=t: e.tensor_scalar(wt, bb[:, L, :], cst[:, 2, t:t + 1], None,
                                                                      ALU.mult))
                        op("dve", lambda e, acc=acc: e.tensor_tensor(wu, acc, wt, ALU.add))
                        op("dve", lambda e: e.tensor_scalar(gt, wu, 0.0, None, ALU.max))
                        turned(t)
                        continue
                    op("sp", lambda e, t=t: e.dma_start(xt[0:rows(t), :], x[t * P:t * P + rows(t), :]), 16)
                    op("dve", lambda e, t=t, acc=acc: e.scalar_tensor_tensor(wt, acc, cst[:, 3, t:t + 1],
                                                                             bb[:, 2, :], ALU.mult, ALU.add))
                    op("dve", lambda e: e.tensor_tensor(wu, wt, xt, ALU.add))
                    ln = lnb[:, 0, :]
                    op("dve", lambda e: e.bn_stats(ln[:, 0:6], wu))
                    op("dve", lambda e: e.bn_aggr(ln[:, 6:8], ln[:, 0:6]))
                    op("dve", lambda e: e.tensor_scalar(ln[:, 7:8], ln[:, 7:8], EPS, None, ALU.add))
                    op("act", lambda e: e.activation(ln[:, 8:9], ln[:, 7:8], ACT.Sqrt))
                    op("dve", lambda e: e.reciprocal(ln[:, 9:10], ln[:, 8:9]))
                    op("dve", lambda e: e.scalar_tensor_tensor(ln[:, 10:11], ln[:, 9:10], ln[:, 7:8], ln[:, 8:9],
                                                               ALU.mult, ALU.add))
                    op("dve", lambda e: e.reciprocal(ln[:, 11:12], ln[:, 10:11]))
                    op("dve", lambda e: e.tensor_scalar(ln[:, 9:10], ln[:, 11:12], 2.0, None, ALU.mult))
                    op("dve", lambda e: e.tensor_scalar(gt, wu, ln[:, 6:7], ln[:, 9:10], ALU.subtract, ALU.mult))
                    op("sp", lambda e, t=t: e.dma_start(out[t * P:t * P + rows(t), :], gt[0:rows(t), :]), 16)

    def run(eng, name):
        turn = 0
        for n, (who, fn, inc) in enumerate(line):
            if n == 0:
                if name == who:
                    fn(eng)
                turn = 1
                continue
            if who == "loop":
                if name in fn:
                    eng.wait_ge(S["s_turn"], turn)
                    with eng.Fori(0, NCH) as i:
                        fn[name](eng, i, inc * NCH)
                    if name == "pe":
                        eng.wait_ge(S["s_ld"], (inc + 1) * NCH + 1)
                        eng.sem_inc(S["s_turn"], 1)
                turn += 1
                continue
            if who == name:
                eng.wait_ge(S["s_turn"], turn)
                fn(eng).then_inc(S["s_turn"], inc)
            turn += inc
        eng.wait_ge(S["s_turn"], turn)

    return run


def bass_tag_gnn_layernorm(nc, x, table, heads, edges, Ws, bs, vd, out):
    SCHED = schedule()
    pe_no, v_no, t_no = {}, {}, {}
    for it in SCHED:
        if it[0] == "T":
            t_no[it[1:]] = len(t_no)
        else:
            pe_no[it[1:]] = len(pe_no)
            if it[2] > 0:
                v_no[it[1:]] = len(v_no)
    vbuf = {(L, k): (L + 3 - k) % 2 for L in range(3) for k in (3, 2, 1)}

    with ExitStack() as ctx:
        def sb(name, shape, dt):
            return ctx.enter_context(nc.sbuf_tensor(name, shape, dt))

        def ps(name, shape, dt):
            return ctx.enter_context(nc.psum_tensor(name, shape, dt))

        def sem(name):
            return ctx.enter_context(nc.semaphore(name))

        A8 = sb("A8", [P, NT, NP], F8)
        V = [sb(f"V{i}", [P, NT, 512], F16) for i in range(2)]
        gT = sb("gT", [P, NT, 2, 2, P], F16)
        Whl = sb("Whl", [P, 3, 2, 4, 512], F16)
        bb = sb("bb", [P, 3, F], F32)
        identf = sb("identf", [P, P], F32)
        iotaB = sb("iotaB", [P, P], F16)
        iotaK = sb("iotaK", [P, KEYS + 1], F16)
        ones16 = sb("ones16", [P, 2], F16)
        thr = sb("thr", [P, 2, NQ], F32)
        cnt = sb("cnt", [P, 4], F32)
        idx = sb("idx", [P, 4], I32)
        dg = sb("dg", [P, 8, NT], F32)
        cst = sb("cst", [P, 5, NT], F32)
        xr = sb("xr", [P, RB, F], F32)
        t1 = sb("t1", [P, RB, F], F32)
        t2 = sb("t2", [P, 2, F], F32)
        w = sb("w", [P, RB, F], F32)
        g = sb("g", [P, RB, F], F32)
        lnb = sb("lnb", [P, RB, 12], F32)
        epst = sb("epst", [P, 2], F32)
        stat = sb("stat", [P, 12 * NT + 3], F32)
        ast = sb("ast", [P, NAM], F32)
        chk = sb("chk", [P, 40], F32)
        want = sb("want", [1, 4], F32)
        flag = sb("flag", [1, 2], I32)
        onesf = sb("onesf", [P, 2], F32)

        Wraw = V[0][:, :, :].rearrange("p a b -> p (a b)")[:, 0:12288].bitcast(F32).rearrange(
            "p (l c k n) -> p l c k n", l=3, c=2, k=4)
        v1 = V[1][:, :, :].rearrange("p a b -> p (a b)")
        Wsc = v1[:, 0:4096].bitcast(F32).rearrange("p (m n) -> p m n", m=8)
        KB = v1[:, 4096:4096 + 2 * NQ * 4 * BG].bitcast(F32).rearrange("p (q m e) -> p q m e", q=NQ, m=4)
        oh = v1[:, 6400:6400 + NR * 404].rearrange("p (r e) -> p r e", r=NR)
        g1 = gT[:, :, :, :, :].rearrange("p a b c d -> p (a b c d)")
        H = g1[:, 0:6250].bitcast(I32)
        junk = g1[:, 6256:6256 + N]
        G = g1[:, 9472:9472 + 3072].bitcast(I32).rearrange("p (q s e) -> p q s e", q=NQ, s=2)
        tmi = w[:, 0:2, :]
        tmf = t1

        bank = [ps(f"pb{i}", [P, 512], F32) for i in range(8)]
        PB = bank[0:NB]
        TB = bank[NB:NB + 2]
        DG = bank[7]

        names = ("s_h s_w s_b s_cst s_cnt s_idx s_gat s_wk s_ki s_kt s_kb s_oh s_vis s_ev s_deg s_dg s_sq s_cs "
                 "s_whi s_wp s_x s_ps s_a1 s_d1 s_a2 s_v s_gx s_g s_tp s_th s_tl s_z s_ln s_sd s_o s_dd s_st s_ck s_pk s_flag s_turn s_lp s_ld s_pl").split()
        S = {n: sem(n) for n in names}
        s_xl = [sem(f"s_xl{i}") for i in range(RB)]
        s_ol = [sem(f"s_ol{i}") for i in range(RB)]
        s_msg = [sem(f"s_msg{i}") for i in range(9 * NQ)]
        s_gl = [sem(f"s_gl{i}") for i in range(NQ)]
        block = ctx.enter_context(nc.Block())
        general = general_path(nc, x, edges, Ws, bb, vd, out, A8, bank, cst, dg, w, g, lnb, identf, onesf, S, s_msg)

        def ending(eng, name):
            eng.wait_ge(S["s_flag"], 1)
            bad = eng.value_load(flag[0:1, 0:1], min_val=0, max_val=1)
            with eng.If(bad != 0):
                general(eng, name)


        def deg_after(t):
            return min(NG - 1, (P * (t + 1) - 1) // GW)

        @block.sync
        def _(sp):
            def store(t):
                sp.wait_ge(S["s_o"], t + 1)
                sp.dma_start(out[t * P:t * P + rows(t), :], g[0:rows(t), t % RB, :]).then_inc(s_ol[t % RB], 16)

            sp.dma_start(H[0:BG, :], heads.rearrange("(a n) -> a n", a=1).broadcast_to([BG, N])).then_inc(S["s_h"], 16)
            for L in range(3):
                for c in range(2):
                    sp.dma_start(Wraw[:, L, c, :, :], Ws[L][:, c * P:(c + 1) * P, :].rearrange("k f n -> f k n"))\
                      .then_inc(S["s_w"], 16)
            for L in range(3):
                sp.dma_start(bb[:, L, :], bs[L].rearrange("(a n) -> a n", a=1).broadcast_to([P, F])).then_inc(S["s_b"], 16)
            for i in range(2 * NT):
                t = i % NT
                if i >= RB:
                    if i - RB < NT:
                        sp.wait_ge(S["s_gx"], i - RB + 1)
                    else:
                        sp.wait_ge(S["s_z"], i - RB - NT + 1)
                sp.dma_start(xr[0:rows(t), i % RB, :], x[t * P:t * P + rows(t), :]).then_inc(s_xl[i % RB], 16)
                if i - NT - RB >= 0:
                    store(i - NT - RB)
            for t in range(NT - RB, NT):
                store(t)
            for i in range(RB):
                sp.wait_ge(s_ol[i], 16 * len(range(i, NT, RB)))
            ending(sp, "sp")

        @block.gpsimd
        def _(pool):
            pool.memset(identf[:, :], 0.0).then_inc(S["s_cst"], 1)
            pool.iota(thr[:, 0, :], pattern=[[GW * BG, NQ]], base=0, channel_multiplier=GW,
                      allow_small_or_imprecise_dtypes=True).then_inc(S["s_cst"], 1)
            pool.iota(thr[:, 1, :], pattern=[[GW * BG, NQ]], base=5, channel_multiplier=GW,
                      allow_small_or_imprecise_dtypes=True).then_inc(S["s_cst"], 1)
            pool.iota(iotaB[:, :], pattern=[[1, P]], base=0, channel_multiplier=0,
                      allow_small_or_imprecise_dtypes=True).then_inc(S["s_cst"], 1)
            pool.iota(iotaK[:, :], pattern=[[1, KEYS + 1]], base=-5, channel_multiplier=0,
                      allow_small_or_imprecise_dtypes=True).then_inc(S["s_cst"], 1)
            pool.memset(ones16[:, :], 1.0).then_inc(S["s_cst"], 1)
            pool.memset(epst[:, :], EPS).then_inc(S["s_cst"], 1)
            pool.memset(want[:, 0:1], float(E)).then_inc(S["s_cst"], 1)
            pool.memset(want[:, 1:2], 0.0).then_inc(S["s_cst"], 1)
            pool.memset(want[:, 2:3], 15.0).then_inc(S["s_cst"], 1)
            pool.memset(onesf[:, :], 1.0).then_inc(S["s_cst"], 1)
            pool.memset(A8[:, :, (NG - 1) * GW:NP], 0.0).then_inc(S["s_cst"], 1)
            pool.wait_ge(S["s_cst"], 1)
            pool.affine_select(out=identf[:, :], in_=identf[:, :], compare_op=ALU.not_equal, fill=1.0, base=0,
                               pattern=[[-1, P]], channel_multiplier=1).then_inc(S["s_cst"], 1)
            for q in range(NQ):
                pool.wait_ge(S["s_idx"], q + 1)
                pool.indirect_dma_start(G[0:BG, q, :, :].rearrange("p s e -> p (s e)"), None, table[:, :],
                                        bass.IndirectOffsetOnAxis(ap=idx[0:BG, q:q + 1], axis=0)).then_inc(s_gl[q], 16)
            for L in range(3):
                raw = Wraw[:, L].rearrange("p c k n -> p (c k) n")
                sc = Wsc
                hl = Whl[:, L].rearrange("p c k n -> p (c k) n")
                if L == 0:
                    pool.wait_ge(S["s_w"], 96)
                else:
                    pool.wait_ge(S["s_wp"], 3 * L)
                pool.tensor_scalar(sc, raw, SV * SC, None, ALU.mult).then_inc(S["s_wp"], 1)
                pool.wait_ge(S["s_whi"], L + 1)
                pool.wait_ge(S["s_wp"], 3 * L + 1)
                pool.tensor_scalar(raw, hl[:, :, 0:F], SC, None, ALU.mult).then_inc(S["s_wp"], 1)
                pool.wait_ge(S["s_wp"], 3 * L + 2)
                pool.tensor_tensor(hl[:, :, F:512], sc, raw, ALU.subtract).then_inc(S["s_wp"], 1)
            ending(pool, "pool")

        @block.scalar
        def _(act):
            act.wait_ge(S["s_w"], 96)
            for L in range(3):
                act.activation(Whl[:, L].rearrange("p c k n -> p (c k) n")[:, :, 0:F],
                               Wraw[:, L].rearrange("p c k n -> p (c k) n"), ACT.Copy, scale=SV).then_inc(S["s_whi"], 1)
            act.wait_ge(S["s_cst"], 12)
            for gi in range(NG):
                n = min(GW, N - gi * GW)
                act.wait_ge(S["s_vis"], gi + 1)
                act.activation(A8[:, :, gi * GW:gi * GW + n],
                               bank[gi % SB_][:, 0:KEYS].rearrange("p (a w) -> p a w", w=GW)[:, :, 0:n],
                               ACT.Copy, saturate=False).then_inc(S["s_ev"], 1)
            act.wait_ge(S["s_dg"], 2)
            act.activation(dg[:, 2, :], dg[:, 1, :], ACT.Sqrt).then_inc(S["s_sq"], 1)
            act.wait_ge(S["s_cs"], 1)

            def g_first(t):
                r = rows(t)
                act.wait_ge(s_xl[t % RB], 16 * (t // RB + 1))
                if t >= RB:
                    act.wait_ge(S["s_tp"], t - RB + 1)
                act.activation(g[:, t % RB, :], xr[:, t % RB, :], ACT.Copy,
                               scale=cst[:, 2, t:t + 1]).then_inc(S["s_gx"], 1)

            g_first(0)
            g_first(1)
            g_first(2)
            for it in SCHED:
                if it[0] == "T":
                    _, L, t = it
                    j = t_no[(L, t)]
                    act.wait_ge(S["s_tp"], j + 1)
                    act.activation(gT[:, t, :, 0, :], TB[j % 2][:, 0:F].rearrange("p (c m) -> p c m", c=2),
                                   ACT.Copy, scale=1.0 / SC).then_inc(S["s_th"], 1)
                    if L == 0 and t + 3 < NT:
                        g_first(t + 3)
                    continue
                _, L, k, t = it
                e = pe_no[(L, k, t)]
                act.wait_ge(S["s_ps"], e + 1)
                if e >= RB:
                    act.wait_ge(S["s_d1"], e - RB + 1)
                lo = PB[e % NB][:, F:512]
                if k > 0:
                    sc = cst[:, 0, t:t + 1]
                elif L < 2:
                    sc = 1.0 / SV
                else:
                    sc = cst[:, 4, t:t + 1]
                act.activation(t1[:, e % RB, :], lo, ACT.Copy, scale=sc).then_inc(S["s_a1"], 1)
                if k > 0:
                    v = v_no[(L, k, t)]
                    act.wait_ge(S["s_d1"], e + 1)
                    act.activation(V[vbuf[(L, k)]][:, t, 0:F], w[:, e % RB, :], ACT.Copy,
                                   scale=1.0 / SC).then_inc(S["s_a2"], 1)
                elif L == 2:
                    act.wait_ge(S["s_ln"], t + 1)
                    act.activation(lnb[:, t % RB, 8:9], lnb[:, t % RB, 7:8], ACT.Sqrt).then_inc(S["s_sd"], 1)
            ending(act, "act")

        @block.tensor
        def _(pe):
            pe.wait_ge(S["s_cst"], 13)
            done = 0

            def degree(t):
                pe.wait_ge(S["s_ev"], deg_after(t) + 1)
                for a in range(NT):
                    mm = pe.matmul(DG[:, t:t + 1], A8[:, a, t * P:(t + 1) * P], ones16[:, 0:1],
                                   start=(a == 0), stop=(a == NT - 1))
                mm.then_inc(S["s_deg"], 1)

            for q in range(NQ):
                pe.wait_ge(S["s_ki"], q + 1)
                for m in range(4):
                    src = tmf[0:BG, 2 + m // 2, (m % 2) * P:(m % 2 + 1) * P]
                    mm = pe.transpose(bank[6][:, m * P:m * P + BG], src, identf[0:BG, 0:BG])
                mm.then_inc(S["s_kt"], 1)
                for gl in range(BG):
                    gi = q * BG + gl
                    if gi >= SB_:
                        pe.wait_ge(S["s_ev"], gi - SB_ + 1)
                    for k in range(2):
                        vis = 2 * gi + k
                        pe.wait_ge(S["s_oh"], vis + 1)
                        mm = pe.matmul(bank[gi % SB_][:, 0:KEYS], oh[:, vis % NR, 0:P],
                                       oh[:, vis % NR, P:P + KEYS], start=(k == 0), stop=(k == 1))
                    mm.then_inc(S["s_vis"], 1)
                    if done < NT - 1 and gi >= deg_after(done) + 5:
                        degree(done)
                        done += 1
            while done < NT:
                degree(done)
                done += 1
            pe.wait_ge(S["s_wp"], 9)
            for it in SCHED:
                if it[0] == "T":
                    _, L, t = it
                    j = t_no[(L, t)]
                    if L == 0:
                        pe.wait_ge(S["s_gx"], t + 1)
                    else:
                        pe.wait_ge(S["s_g"], j - NT + 1)
                    if j >= 2:
                        pe.wait_ge(S["s_tl"], j - 1)
                    for c in range(2):
                        mm = pe.transpose(TB[j % 2][:, c * P:(c + 1) * P], g[:, j % RB, c * P:(c + 1) * P],
                                          identf[:, :])
                    mm.then_inc(S["s_tp"], 1)
                    continue
                _, L, k, t = it
                e = pe_no[(L, k, t)]
                if e >= NB:
                    pe.wait_ge(S["s_d1"], e - NB + 1)
                if k == 3:
                    pe.wait_ge(S["s_tl"], t_no[(L, t)] + 1)
                acc = PB[e % NB]
                for c in range(2):
                    pe.matmul(acc[:, :], gT[:, t, c, 0, :], Whl[:, L, c, k, :], start=(c == 0), stop=False,
                              skip_group_check=True)
                    mm = pe.matmul(acc[:, F:512], gT[:, t, c, 1, :], Whl[:, L, c, k, 0:F], start=False,
                                   stop=(k == 3 and c == 1), skip_group_check=True)
                if k < 3:
                    src = V[vbuf[(L, k + 1)]]
                    for a in range(NT):
                        if t == 0:
                            pe.wait_ge(S["s_v"], v_no[(L, k + 1, a)] + 1)
                        mm = pe.matmul(acc[:, :], A8[:, a, t * P:(t + 1) * P], src[:, a, :], start=False,
                                       stop=(a == NT - 1), skip_group_check=True)
                mm.then_inc(S["s_ps"], 1)
                if (L, k, t) == (2, 0, 13):
                    pe.wait_ge(S["s_ck"], 1)
                    pe.transpose(bank[7][0:15, 0:P], chk[:, 0:15], identf[:, :]).then_inc(S["s_pk"], 1)
                if (L, k, t) == (2, 0, 18):
                    pe.wait_ge(S["s_ck"], 2)
                    pe.matmul(bank[7][0:1, 128:130], onesf[:, 0:1], chk[:, 15:17], start=True, stop=True)
                    pe.matmul(bank[7][0:1, 130:131], onesf[0:15, 0:1], chk[0:15, 21:22], start=True,
                              stop=True).then_inc(S["s_pk"], 1)
            ending(pe, "pe")

        @block.vector
        def _(dve):
            H16 = H.bitcast(I16).rearrange("p (n two) -> p n two", two=2)[:, :, 0]
            dve.wait_ge(S["s_h"], 16)
            dve.wait_ge(S["s_cst"], 3)
            for q in range(NQ):
                dve.tensor_scalar(junk[0:BG, :], H16[0:BG, :], thr[0:BG, 0, q:q + 1], None, ALU.is_lt, ALU.add,
                                  accum_out=cnt[0:BG, q:q + 1]).then_inc(S["s_cnt"], 1)
                dve.wait_ge(S["s_cnt"], q + 1)
                dve.tensor_scalar(idx[0:BG, q:q + 1], cnt[0:BG, q:q + 1], -1.0, 0.0, ALU.add,
                                  ALU.max).then_inc(S["s_idx"], 1)
            kk = 0

            def link(ins):
                nonlocal kk
                kk += 1
                ins.then_inc(S["s_wk"], 1)
                dve.wait_ge(S["s_wk"], kk)

            dve.wait_ge(S["s_cst"], 13)
            for q in range(NQ):
                dve.wait_ge(s_gl[q], 16)
                s_, d_ = G[0:BG, q, 0, :], G[0:BG, q, 1, :]
                ai = w[0:BG, 0, :].bitcast(I32)
                bi = w[0:BG, 1, :].bitcast(I32)
                dl, sq = w[0:BG, 2, :], w[0:BG, 3, :]
                if q:
                    dve.wait_ge(S["s_kt"], q)
                link(dve.tensor_scalar(ai, s_, 7, None, ALU.logical_shift_right))
                link(dve.tensor_scalar(bi, s_, P - 1, None, ALU.bitwise_and))
                link(dve.tensor_copy(t1[0:BG, 3, :], bi))
                link(dve.tensor_scalar(dl, d_, thr[0:BG, 1, q:q + 1], None, ALU.subtract))
                link(dve.tensor_tensor(sq, dl, dl, ALU.mult))
                link(dve.tensor_scalar(t1[0:BG, 0, :], sq, 25.5, 1000.0, ALU.is_gt, ALU.mult))
                link(dve.scalar_tensor_tensor(t1[0:BG, 1, :], ai, float(GW), dl, ALU.mult, ALU.add))
                dve.tensor_tensor(t1[0:BG, 2, :], t1[0:BG, 0, :], t1[0:BG, 1, :], ALU.add).then_inc(S["s_ki"], 1)
                dve.wait_ge(S["s_kt"], q + 1)
                dve.tensor_copy(KB[:, q, :, :], bank[6][:, :].rearrange("p (m e) -> p m e", m=4)[:, :, 0:BG])\
                   .then_inc(S["s_kb"], 1)
                dve.wait_ge(S["s_kb"], q + 1)
                for gl in range(BG):
                    gi = q * BG + gl
                    for k in range(2):
                        vis = 2 * gi + k
                        if vis >= NR:
                            dve.wait_ge(S["s_vis"], (vis - NR) // 2 + 1)
                        dve.tensor_scalar(oh[:, vis % NR, 0:P], iotaB[:, :], KB[:, q, 2 + k, gl:gl + 1], None,
                                          ALU.is_equal)
                        dve.tensor_scalar(oh[:, vis % NR, P:P + KEYS], iotaK[:, 0:KEYS], KB[:, q, k, gl:gl + 1],
                                          None, ALU.is_equal).then_inc(S["s_oh"], 1)
            nd = 0

            def dl_(ins):
                nonlocal nd
                nd += 1
                ins.then_inc(S["s_dd"], 1)
                dve.wait_ge(S["s_dd"], nd)

            dve.wait_ge(S["s_deg"], NT)
            dve.tensor_copy(dg[:, 0, :], DG[:, 0:NT]).then_inc(S["s_dg"], 1)
            dve.wait_ge(S["s_dg"], 1)
            dve.tensor_scalar(dg[:, 1, :], dg[:, 0, :], 1.0, None, ALU.max).then_inc(S["s_dg"], 1)
            dve.wait_ge(S["s_dg"], 2)
            dl_(dve.reciprocal(dg[:, 3, :], dg[:, 1, :]))
            dl_(dve.tensor_scalar(dg[:, 4, :], dg[:, 0, :], 1.0, None, ALU.min))
            dl_(dve.tensor_tensor(cst[:, 0, :], dg[:, 3, :], dg[:, 4, :], ALU.mult))
            dl_(dve.tensor_scalar(cst[:, 1, :], cst[:, 0, :], SC, None, ALU.mult))
            dve.wait_ge(S["s_sq"], 1)
            dl_(dve.reciprocal(dg[:, 5, :], dg[:, 2, :]))
            dl_(dve.tensor_tensor(dg[:, 6, :], dg[:, 5, :], dg[:, 1, :], ALU.mult))
            dl_(dve.tensor_tensor(dg[:, 7, :], dg[:, 6, :], dg[:, 2, :], ALU.add))
            dl_(dve.tensor_scalar(cst[:, 2, :], dg[:, 7, :], 0.5 * SC, None, ALU.mult))
            dl_(dve.reciprocal(dg[:, 5, :], dg[:, 7, :]))
            dl_(dve.tensor_scalar(cst[:, 3, :], dg[:, 5, :], 2.0 / SV, None, ALU.mult))
            dve.tensor_scalar(cst[:, 4, :], dg[:, 5, :], 2.0 / (SV * SC), None, ALU.mult).then_inc(S["s_cs"], 1)
            dve.wait_ge(S["s_cs"], 1)
            dve.wait_ge(S["s_b"], 48)
            nst = nam = 0
            dve.wait_ge(S["s_whi"], 3)
            for L in range(3):
                dve.tensor_reduce(stat[:, 12 * NT + L:12 * NT + L + 1],
                                  Whl[:, L].rearrange("p c k n -> p (c k) n")[:, :, 0:F], AX.XY, ALU.max,
                                  apply_absolute_value=True).then_inc(S["s_st"], 1)
                nst += 1

            def verdict(part):
                if part == 0:
                    verdict_maxima()
                elif part == 1:
                    verdict_ranges()
                else:
                    dve.wait_ge(S["s_pk"], 2)
                    dl_(dve.tensor_copy(chk[0:1, 24:27], bank[7][0:1, 128:131]))
                    dl_(dve.tensor_tensor(chk[0:1, 28:31], chk[0:1, 24:27], want[:, 0:3], ALU.not_equal))
                    dve.tensor_reduce(flag[:, 0:1], chk[0:1, 28:31], AX.X, ALU.max).then_inc(S["s_flag"], 1)

            def verdict_maxima():
                assert nam == NAM
                dve.wait_ge(S["s_st"], nst)
                dl_(dve.tensor_reduce(chk[:, 0:12], stat[:, 0:12 * NT].rearrange("p (m t) -> p m t", t=NT), AX.X,
                                      ALU.max))
                dl_(dve.tensor_copy(chk[:, 12:15], stat[:, 12 * NT:12 * NT + 3]))
                dl_(dve.tensor_reduce(chk[:, 15:16], dg[:, 0, :], AX.X, ALU.add))
                dl_(dve.tensor_reduce(chk[:, 17:18], ast[:, :], AX.X, ALU.max))
                dve.tensor_scalar(chk[:, 16:17], chk[:, 17:18], AMAX, None, ALU.is_ge).then_inc(S["s_ck"], 1)

            def verdict_ranges():
                dve.wait_ge(S["s_pk"], 1)
                dl_(dve.tensor_reduce(chk[0:15, 18:19], bank[7][0:15, 0:P], AX.X, ALU.max))
                dl_(dve.tensor_scalar(chk[0:15, 19:20], chk[0:15, 18:19], LOW, None, ALU.is_ge))
                dl_(dve.tensor_scalar(chk[0:15, 20:21], chk[0:15, 18:19], HIGH, None, ALU.is_le))
                dve.tensor_tensor(chk[0:15, 21:22], chk[0:15, 19:20], chk[0:15, 20:21],
                                  ALU.mult).then_inc(S["s_ck"], 1)

            for it in SCHED:
                if it[0] == "T":
                    _, L, t = it
                    j = t_no[(L, t)]
                    dve.wait_ge(S["s_th"], j + 1)
                    dve.scalar_tensor_tensor(gT[:, t, :, 1, :], gT[:, t, :, 0, :], -SC,
                                             TB[j % 2][:, 0:F].rearrange("p (c m) -> p c m", c=2),
                                             ALU.mult, ALU.add).then_inc(S["s_tl"], 1)
                    dve.tensor_reduce(stat[:, 9 * NT + j:9 * NT + j + 1], gT[:, t, :, 0, :], AX.XY, ALU.max,
                                      apply_absolute_value=True).then_inc(S["s_st"], 1)
                    nst += 1
                    continue
                _, L, k, t = it
                e = pe_no[(L, k, t)]
                hi = PB[e % NB][:, 0:F]
                we = w[:, e % RB, :]
                if k > 0:
                    dve.wait_ge(S["s_a1"], e + 1)
                    v = v_no[(L, k, t)]
                    vb = V[vbuf[(L, k)]]
                    dve.scalar_tensor_tensor(we, hi, cst[:, 1, t:t + 1], t1[:, e % RB, :], ALU.mult,
                                             ALU.add).then_inc(S["s_d1"], 1)
                    dve.wait_ge(S["s_a2"], v + 1)
                    dve.scalar_tensor_tensor(vb[:, t, F:512], vb[:, t, 0:F], -SC, we, ALU.mult,
                                             ALU.add).then_inc(S["s_v"], 1)
                    dve.tensor_reduce(stat[:, v:v + 1], vb[:, t, 0:F], AX.X, ALU.max,
                                      apply_absolute_value=True).then_inc(S["s_st"], 1)
                    nst += 1
                    if k < 3 and nam < NAM:
                        a_, i_ = nam // 5, nam % 5
                        dve.tensor_reduce(ast[:, nam:nam + 1], A8[:, a_, 640 * i_:640 * i_ + 640].bitcast(U8), AX.X,
                                          ALU.max).then_inc(S["s_st"], 1)
                        nam += 1
                        nst += 1
                elif L < 2:
                    j = t_no[(L + 1, t)]
                    dve.wait_ge(S["s_a1"], e + 1)
                    dl_(dve.scalar_tensor_tensor(t2[:, t % 2, :], bb[:, L, :], cst[:, 2, t:t + 1],
                                                 t1[:, e % RB, :], ALU.mult, ALU.add))
                    dve.scalar_tensor_tensor(we, hi, SC / SV, t2[:, t % 2, :], ALU.mult,
                                             ALU.add).then_inc(S["s_d1"], 1)
                    dve.wait_ge(S["s_d1"], e + 1)
                    dve.wait_ge(S["s_tp"], j - RB + 1)
                    dve.tensor_scalar(g[:, j % RB, :], we, 0.0, None, ALU.max).then_inc(S["s_g"], 1)
                else:
                    i = NT + t
                    if t in (10, 15, 20):
                        verdict((t - 10) // 5)
                    dve.wait_ge(s_xl[i % RB], 16 * (i // RB + 1))
                    r = rows(t)
                    dve.tensor_tensor(t2[:, t % 2, :], xr[:, i % RB, :], bb[:, 2, :], ALU.add).then_inc(S["s_z"], 1)
                    dve.wait_ge(S["s_a1"], e + 1)
                    dve.scalar_tensor_tensor(we, hi, cst[:, 3, t:t + 1], t1[:, e % RB, :], ALU.mult,
                                             ALU.add).then_inc(S["s_d1"], 1)
                    dve.wait_ge(S["s_d1"], e + 1)
                    dve.wait_ge(S["s_z"], t + 1)
                    dl_(dve.tensor_tensor(we, we, t2[:, t % 2, :], ALU.add))
                    ln = lnb[:, t % RB, :]
                    dl_(dve.bn_stats(ln[:, 0:6], we))
                    dl_(dve.bn_aggr(ln[:, 6:8], ln[:, 0:6]))
                    dve.tensor_scalar(ln[:, 7:8], ln[:, 7:8], EPS, None, ALU.add).then_inc(S["s_ln"], 1)
                    dve.wait_ge(S["s_sd"], t + 1)
                    dl_(dve.reciprocal(ln[:, 9:10], ln[:, 8:9]))
                    dl_(dve.scalar_tensor_tensor(ln[:, 10:11], ln[:, 9:10], ln[:, 7:8], ln[:, 8:9], ALU.mult, ALU.add))
                    dl_(dve.reciprocal(ln[:, 11:12], ln[:, 10:11]))
                    dl_(dve.tensor_scalar(ln[:, 9:10], ln[:, 11:12], 2.0, None, ALU.mult))
                    if t >= RB:
                        dve.wait_ge(s_ol[t % RB], 16 * (t // RB))
                    dve.tensor_scalar(g[:, t % RB, :], we, ln[:, 6:7], ln[:, 9:10], ALU.subtract,
                                      ALU.mult).then_inc(S["s_o"], 1)
            ending(dve, "dve")


def kernel(**inputs):
    import numpy as _np
    import concourse.bacc as _bacc
    from concourse import mybir as _mybir
    from concourse.bass_utils import run_bass_kernel_spmd as _run

    nc = _bacc.Bacc("TRN2", target_bir_lowering=False, num_devices=1)
    src = _np.asarray(inputs["src"])
    dst = _np.asarray(inputs["dst"])
    pad = _np.full(WIN, -1, _np.int32)
    srcp = _np.concatenate([src, pad])
    dstp = _np.concatenate([dst, pad])
    at = _np.arange(0, E, GRAN)[:, None] + _np.arange(WIN)[None, :]
    arrays = {"x": _np.ascontiguousarray(inputs["x"]),
              "table": _np.ascontiguousarray(_np.concatenate([srcp[at], dstp[at]], axis=1)),
              "edges": _np.ascontiguousarray(_np.stack([_np.concatenate([src, _np.zeros(NCH * P - E, _np.int32)]),
                                                        dstp[:NCH * P]]).reshape(2, P, NCH)),
              "heads": _np.ascontiguousarray(dst[::GRAN])}
    for i in (1, 2, 3):
        arrays[f"W{i}"] = _np.ascontiguousarray(inputs[f"L0_gnn_W{i}"])
        arrays[f"b{i}"] = _np.ascontiguousarray(inputs[f"L0_gnn_b{i}"])
    ap = {k: nc.dram_tensor("in_" + k, v.shape, _mybir.dt.from_np(v.dtype), kind="ExternalInput").ap()
          for k, v in arrays.items()}
    out = nc.dram_tensor("out_0", (N, F), _mybir.dt.float32, kind="ExternalOutput").ap()
    vd = [nc.dram_tensor(f"vd{i}", (NP, F), _mybir.dt.float32, kind="Internal").ap() for i in range(2)]
    bass_tag_gnn_layernorm(nc, ap["x"], ap["table"], ap["heads"], ap["edges"], [ap["W1"], ap["W2"], ap["W3"]],
                           [ap["b1"], ap["b2"], ap["b3"]], vd, out)
    r = _run(nc, [{"in_" + k: v for k, v in arrays.items()}], core_ids=[0])
    return r.results[0]["out_0"]
```

```python
from contextlib import ExitStack

import concourse.bass as bass
from concourse import mybir

P = 128
N = 3125
E = 50000
F = 256
NT = 25
NP = NT * P
TAIL = N - (NT - 1) * P
GW = 11
NG = 285
BG = 95
NQ = 3
KEYS = NT * GW
WIN = 256
GRAN = 16
NR = 11
BV = 8
NO = 3
FAR = 10000.0
RB = 4
SC = 2048.0
SV = 16.0
EPS = 1e-5
HALF = 64
XL = 2 * NT + 16
NCH = -(-E // P)
PT = 9
LOW = 2.0 ** -10
HIGH = 60000.0
AMAX = 87.5
NAM = 4 * NT

ALU = mybir.AluOpType
ACT = mybir.ActivationFunctionType
AX = mybir.AxisListType
F32 = mybir.dt.float32
F16 = mybir.dt.float16
F8 = mybir.dt.float8e4
I32 = mybir.dt.int32
I16 = mybir.dt.int16
U8 = mybir.dt.uint8


def rows(t):
    return P if t < NT - 1 else TAIL


def schedule():
    out = [("T", 0, 0), ("T", 0, 1)]
    for t in range(NT):
        if t + 2 < NT:
            out.append(("T", 0, t + 2))
        out.append(("P", 0, 3, t))
    for L in range(3):
        for k in (2, 1, 0):
            for t in range(NT):
                out.append(("P", L, k, t))
                if k == 0 and L < 2:
                    if t >= 1:
                        out.append(("T", L + 1, t - 1))
                    if t >= 2:
                        out.append(("P", L + 1, 3, t - 2))
        if L < 2:
            out.append(("T", L + 1, NT - 1))
            out.append(("P", L + 1, 3, NT - 2))
            out.append(("P", L + 1, 3, NT - 1))
    return out


def general_path(nc, x, edges, Ws, bb, vd, out, A8, bank, cst, dg, w, g, lnb, identf, onesf, S, s_msg):
    line = []
    region = A8[:, :, :].rearrange("p a b -> p (a b)")
    at = [0]

    def take(n, dt=F32):
        v = region[:, at[0]:at[0] + 4 * n].bitcast(dt)
        at[0] += 4 * n
        return v

    gTs = take(2 * NP).rearrange("p (c n) -> p c n", c=2)
    Wf = take(2048).rearrange("p (c k n) -> p c k n", c=2, k=4)
    iot = take(PT * P)
    oh = take(PT * P)
    msg = take(F)
    srcI = take(NCH, I32)
    dstI = take(NCH, I32)
    dstF = take(NCH)
    tmI = take(NCH, I32)
    dhi = take(NCH)
    dlo = take(NCH)
    sm = take(16)
    smi = take(4, I32)

    def op(name, fn, inc=1):
        line.append((name, fn, inc))

    def loop(fns, lp):
        line.append(("loop", fns, lp))

    def opened(e):
        e.sem_inc(S["s_ld"], 1)
        e.sem_inc(S["s_turn"], 1)

    op("sp", opened, 0)
    op("sp", lambda e: e.dma_start(srcI, edges[0, :, :]), 16)
    op("sp", lambda e: e.dma_start(dstI, edges[1, :, :]), 16)
    op("pool", lambda e: e.iota(iot, pattern=[[1, PT * P]], base=0, channel_multiplier=0,
                                allow_small_or_imprecise_dtypes=True))
    op("dve", lambda e: e.tensor_copy(dstF, dstI))
    op("dve", lambda e: e.tensor_scalar(tmI, dstI, 7, None, ALU.logical_shift_right))
    op("dve", lambda e: e.tensor_copy(dhi, tmI))
    op("dve", lambda e: e.tensor_scalar(tmI, dstI, P - 1, None, ALU.bitwise_and))
    op("dve", lambda e: e.tensor_copy(dlo, tmI))
    op("dve", lambda e: e.memset(oh, 0.0))
    DG = bank[7]
    op("pe", lambda e: e.matmul(DG[:, 0:NT], oh[:, 0:P], oh[:, 0:NT], start=True, stop=False, skip_group_check=True))
    loops = [0]

    def deg_dve(e, i, n0):
        e.wait_ge(S["s_ld"], i + n0 + 1)
        e.tensor_scalar(oh[:, 0:P], iot[:, 0:P], dlo[:, bass.ds(i, 1)], None, ALU.is_equal)
        e.tensor_scalar(oh[:, P:P + NT], iot[:, 0:NT], dhi[:, bass.ds(i, 1)], None,
                        ALU.is_equal).then_inc(S["s_lp"], 1)

    def deg_pe(e, i, n0):
        e.wait_ge(S["s_lp"], i + n0 + 1)
        e.matmul(DG[:, 0:NT], oh[:, 0:P], oh[:, P:P + NT], start=False, stop=False,
                 skip_group_check=True).then_inc(S["s_ld"], 1)

    loop({"dve": deg_dve, "pe": deg_pe}, 0)
    op("dve", lambda e: e.tensor_copy(dg[:, 0, :], DG[:, 0:NT]))
    op("dve", lambda e: e.tensor_scalar(dg[:, 1, :], dg[:, 0, :], 1.0, None, ALU.max))
    op("act", lambda e: e.activation(dg[:, 2, :], dg[:, 1, :], ACT.Sqrt))
    op("dve", lambda e: e.reciprocal(dg[:, 3, :], dg[:, 1, :]))
    op("dve", lambda e: e.tensor_scalar(dg[:, 4, :], dg[:, 0, :], 1.0, None, ALU.min))
    op("dve", lambda e: e.tensor_tensor(cst[:, 0, :], dg[:, 3, :], dg[:, 4, :], ALU.mult))
    op("dve", lambda e: e.reciprocal(dg[:, 5, :], dg[:, 2, :]))
    op("dve", lambda e: e.tensor_tensor(dg[:, 6, :], dg[:, 5, :], dg[:, 1, :], ALU.mult))
    op("dve", lambda e: e.tensor_tensor(dg[:, 7, :], dg[:, 6, :], dg[:, 2, :], ALU.add))
    op("dve", lambda e: e.tensor_scalar(cst[:, 2, :], dg[:, 7, :], 0.5, None, ALU.mult))
    op("dve", lambda e: e.reciprocal(cst[:, 3, :], cst[:, 2, :]))
    wt, wu = w[:, 0, :], w[:, 1, :]
    gt, xt = g[:, 0, :], g[:, 1, :]

    def turned(t):
        for c in range(2):
            op("pe", lambda e, c=c: e.transpose(bank[6][:, c * P:(c + 1) * P], gt[:, c * P:(c + 1) * P],
                                                identf[:, :]))
        op("dve", lambda e: e.tensor_copy(gTs[:, :, t * P:(t + 1) * P],
                                          bank[6][:, 0:F].rearrange("p (c m) -> p c m", c=2)))

    def project(L, k, t, acc, first):
        for c in range(2):
            op("pe", lambda e, c=c: e.matmul(acc, gTs[:, c, t * P:(t + 1) * P], Wf[:, c, k, :],
                                             start=(first and c == 0), stop=False, skip_group_check=True))

    def v_out(t, acc, b):
        op("dve", lambda e: e.tensor_scalar(wt, acc, cst[:, 0, t:t + 1], None, ALU.mult))
        op("sp", lambda e: e.dma_start(vd[b][t * P:(t + 1) * P, :], wt), 16)

    op("dve", lambda e: e.memset(xt, 0.0))
    for t in range(NT):
        op("sp", lambda e, t=t: e.dma_start(xt[0:rows(t), :], x[t * P:t * P + rows(t), :]), 16)
        op("dve", lambda e, t=t: e.tensor_scalar(gt, xt, cst[:, 2, t:t + 1], None, ALU.mult))
        turned(t)
    for L in range(3):
        for c in range(2):
            op("sp", lambda e, L=L, c=c: e.dma_start(
                Wf[:, c, :, :], Ws[L][:, c * P:(c + 1) * P, :].rearrange("k f n -> f k n")), 16)
        for t in range(NT):
            acc = bank[0][:, 0:F]
            project(L, 3, t, acc, True)
            v_out(t, acc, 1)
        for k in (2, 1, 0):
            for q in range(NQ):
                tiles = list(range(q * PT, min(NT, (q + 1) * PT)))
                accs = {t: bank[(t - q * PT) // 2][:, F * ((t - q * PT) % 2):F * ((t - q * PT) % 2) + F]
                        for t in tiles}
                for t in tiles:
                    project(L, k, t, accs[t], (t - q * PT) % 2 == 0)
                loops[0] += 1

                def hop_dve(e, i, n0, q=q):
                    e.wait_ge(S["s_ld"], i + n0 + 1)
                    e.tensor_copy(smi[:, 0:1], srcI[:, bass.ds(i, 1)])
                    e.tensor_scalar(sm[:, 0:1], dstF[:, bass.ds(i, 1)], float(-q * PT * P), None,
                                    ALU.add).then_inc(S["s_lp"], 1)
                    e.wait_ge(S["s_lp"], 2 * i + n0 + n0 - NCH + 1)
                    e.tensor_scalar(oh, iot, sm[:, 0:1], None, ALU.is_equal).then_inc(S["s_lp"], 1)

                def hop_pool(e, i, n0, ms=s_msg[loops[0] - 1], src=vd[(k + 1) % 2 if k < 2 else 1]):
                    e.wait_ge(S["s_lp"], 2 * i + n0 + n0 - NCH + 1)
                    e.sem_inc(S["s_pl"], 1)
                    e.indirect_dma_start(msg, None, src[:, :],
                                         bass.IndirectOffsetOnAxis(ap=smi[:, 0:1], axis=0)).then_inc(ms, 16)

                def hop_pe(e, i, n0, ms=s_msg[loops[0] - 1], tiles=tiles, accs=accs):
                    e.wait_ge(S["s_lp"], 2 * i + n0 + n0 - NCH + 2)
                    e.wait_ge(ms, i * 16 + 16)
                    for n, t in enumerate(tiles):
                        mm = e.matmul(accs[t], oh[:, n * P:(n + 1) * P], msg, start=False, stop=False,
                                      skip_group_check=True)
                    mm.then_inc(S["s_ld"], 1)

                loop({"dve": hop_dve, "pool": hop_pool, "pe": hop_pe}, loops[0])
                for t in tiles:
                    acc = accs[t]
                    if k > 0:
                        v_out(t, acc, k % 2)
                        continue
                    if L < 2:
                        op("dve", lambda e, L=L, t=t: e.tensor_scalar(wt, bb[:, L, :], cst[:, 2, t:t + 1], None,
                                                                      ALU.mult))
                        op("dve", lambda e, acc=acc: e.tensor_tensor(wu, acc, wt, ALU.add))
                        op("dve", lambda e: e.tensor_scalar(gt, wu, 0.0, None, ALU.max))
                        turned(t)
                        continue
                    op("sp", lambda e, t=t: e.dma_start(xt[0:rows(t), :], x[t * P:t * P + rows(t), :]), 16)
                    op("dve", lambda e, t=t, acc=acc: e.scalar_tensor_tensor(wt, acc, cst[:, 3, t:t + 1],
                                                                             bb[:, 2, :], ALU.mult, ALU.add))
                    op("dve", lambda e: e.tensor_tensor(wu, wt, xt, ALU.add))
                    ln = lnb[:, 0, :]
                    op("dve", lambda e: e.bn_stats(ln[:, 0:6], wu))
                    op("dve", lambda e: e.bn_aggr(ln[:, 6:8], ln[:, 0:6]))
                    op("dve", lambda e: e.tensor_scalar(ln[:, 7:8], ln[:, 7:8], EPS, None, ALU.add))
                    op("act", lambda e: e.activation(ln[:, 8:9], ln[:, 7:8], ACT.Sqrt))
                    op("dve", lambda e: e.reciprocal(ln[:, 9:10], ln[:, 8:9]))
                    op("dve", lambda e: e.scalar_tensor_tensor(ln[:, 10:11], ln[:, 9:10], ln[:, 7:8], ln[:, 8:9],
                                                               ALU.mult, ALU.add))
                    op("dve", lambda e: e.reciprocal(ln[:, 11:12], ln[:, 10:11]))
                    op("dve", lambda e: e.tensor_scalar(ln[:, 9:10], ln[:, 11:12], 2.0, None, ALU.mult))
                    op("dve", lambda e: e.tensor_scalar(gt, wu, ln[:, 6:7], ln[:, 9:10], ALU.subtract, ALU.mult))
                    op("sp", lambda e, t=t: e.dma_start(out[t * P:t * P + rows(t), :], gt[0:rows(t), :]), 16)

    def run(eng, name):
        turn = 0
        for n, (who, fn, inc) in enumerate(line):
            if n == 0:
                if name == who:
                    fn(eng)
                turn = 1
                continue
            if who == "loop":
                if name in fn:
                    eng.wait_ge(S["s_turn"], turn)
                    with eng.Fori(0, NCH) as i:
                        fn[name](eng, i, inc * NCH)
                    if name == "pe":
                        eng.wait_ge(S["s_ld"], (inc + 1) * NCH + 1)
                        eng.sem_inc(S["s_turn"], 1)
                turn += 1
                continue
            if who == name:
                eng.wait_ge(S["s_turn"], turn)
                fn(eng).then_inc(S["s_turn"], inc)
            turn += inc
        eng.wait_ge(S["s_turn"], turn)

    return run


def groups_of(t):
    last = [-1] + [min(NG - 1, (P * (i + 1) - 1) // GW) for i in range(NT)]
    return list(range(last[t] + 1, last[t + 1] + 1)) if t < NT else []


def trailing(sched, empty, split):
    out = []
    held = None
    for it in sched:
        if it[0] == "T":
            out.append(it)
            continue
        L, k, t = it[1:]
        if k == 2 and held:
            out.append(held)
            held = None
        if (L, k) == (0, 2):
            gs = [("B", gi) for gi in groups_of(t + 1)]
            before = ("P", 0, 2, t - 1), ("V", 0, 2, t - 1)
            out += (gs[:empty] + ([before[0]] if t else []) + gs[empty:split] + ([before[1]] if t else [])
                    + gs[split:])
            if t == NT - 1:
                out += [it, ("V",) + it[1:]]
            continue
        out.append(it)
        if held:
            out.append(held)
        held = ("V",) + it[1:] if k > 0 else None
        if held and (L, k) != (0, 3):
            out.append(held)
            held = None
    return out


def bass_tag_gnn_layernorm(nc, x, table, heads, edges, Ws, bs, vd, degd, out):
    SCHED = schedule()
    pe_no, v_no, t_no = {}, {}, {}
    for it in SCHED:
        if it[0] == "T":
            t_no[it[1:]] = len(t_no)
        else:
            pe_no[it[1:]] = len(pe_no)
            if it[2] > 0:
                v_no[it[1:]] = len(v_no)
    p_of = {e: key for key, e in pe_no.items()}
    vbuf = {(L, k): (L + 3 - k) % 2 for L in range(3) for k in (3, 2, 1)}

    with ExitStack() as ctx:
        def sb(name, shape, dt):
            return ctx.enter_context(nc.sbuf_tensor(name, shape, dt))

        def ps(name, shape, dt):
            return ctx.enter_context(nc.psum_tensor(name, shape, dt))

        def sem(name):
            return ctx.enter_context(nc.semaphore(name))

        A8 = sb("A8", [P, NT, NP], F8)
        V = [sb(f"V{i}", [P, NT, 512], F16) for i in range(2)]
        AT = sb("AT", [P, NP], F16)
        gT = sb("gT", [P, NT, 2, 2, P], F16)
        Whl = sb("Whl", [P, 3, 2, 4, 512], F16)
        bb = sb("bb", [P, 3, F], F32)
        identf = sb("identf", [P, P], F32)
        KBk = sb("KBk", [P, 2 * NG], F32)
        thS = sb("thS", [P, NQ + GW + 1], F32)
        cS = sb("cS", [P, NQ + GW + 1], F32)
        dgw = sb("dgw", [BG, NQ, GW], F32)
        dgT = sb("dgT", [NT, P], F32)
        thr = sb("thr", [P, 2, NQ], F32)
        cnt = sb("cnt", [P, 4], F32)
        idx = sb("idx", [P, 4], I32)
        dg = sb("dg", [P, 8, NT], F32)
        cst = sb("cst", [P, 5, NT], F32)
        xr = sb("xr", [P, RB, F], F32)
        t1 = sb("t1", [P, RB, F], F32)
        w = sb("w", [P, RB, F], F32)
        g = sb("g", [P, RB, F], F32)
        lnb = sb("lnb", [P, RB, 12], F32)
        stat = KBk[:, 0:12 * NT + 3]
        ast = KBk[:, 320:320 + NAM]
        chk = sb("chk", [P, 40], F32)
        want = sb("want", [1, 4], F32)
        flag = sb("flag", [1, 2], I32)
        onesf = sb("onesf", [P, 2], F32)

        v1 = V[1][:, :, :].rearrange("p a b -> p (a b)")
        Wraw = v1[:, 0:4096].bitcast(F32).rearrange("p (m n) -> p m n", m=8)
        Wsc = v1[:, 4096:8192].bitcast(F32).rearrange("p (m n) -> p m n", m=8)
        w12 = Whl[:, 1:3, :, :, :].rearrange("p l c k n -> p (l c k n)")
        OB = w12[:, 0:NO * P * BV].rearrange("p (r j v) -> p r j v", r=NO, v=BV)
        OK = w12[:, 3072:3072 + NR * 276].rearrange("p (r e) -> p r e", r=NR)
        iotaK = w12[:, 6108:6108 + KEYS + 1]
        KBb = w12[:, 6384:6384 + 2 * NG + BV]
        iotaB = w12[:, 7168:7168 + P * BV].rearrange("p (j v) -> p j v", v=BV)
        g1 = gT[:, :, :, :, :].rearrange("p a b c d -> p (a b c d)")
        H = g1[:, 0:6250].bitcast(I32)
        junk = g1[:, 6256:6256 + N]
        G = g1[:, 9472:9472 + 3072].bitcast(I32).rearrange("p (q s e) -> p q s e", q=NQ, s=2)
        tmi = w[:, 0:2, :]
        tmf = t1

        bank = [ps(f"pb{i}", [P, 512], F32) for i in range(8)]
        bank_of, free, user = {}, [0, 1, 2, 5, 6], {}
        for e, (L, k, t) in p_of.items():
            few = (L, k) == (0, 2) or (L, k) == (0, 3) and t >= NT - 4
            b = next(i for i in free if not few or i < 5)
            free.remove(b)
            free.append(b)
            bank_of[e] = b
            before = [f for f in range(e) if bank_of[f] == b]
            if before:
                user[e] = before[-1]
        last_init = max(e for e in range(NT) if bank_of[e] > 4)
        PB = [bank[bank_of[e]] for e in range(len(p_of))]
        TB = bank[3:5]
        BB = bank[5:7]

        names = ("s_h s_w s_b s_cst s_cnt s_idx s_gat s_wk s_ki s_kt s_kb s_oh s_vis s_ev s_ob s_dw s_dr s_dz s_dt s_wq s_wi s_deg s_dg s_sq s_cs "
                 "s_whi s_wp s_x s_ps s_a1 s_d1 s_a2 s_v s_gx s_g s_tp s_th s_tl s_z s_ln s_sd s_o s_dd s_st s_ck s_pk s_flag s_turn s_lp s_ld s_pl s_at s_sg s_dl").split()
        S = {n: sem(n) for n in names}
        t2 = w[:, 2:4, :]
        H16 = H.bitcast(I16).rearrange("p (n two) -> p n two", two=2)[:, :, 0]
        s_xl = [sem(f"s_xl{i}") for i in range(RB)]
        s_ol = [sem(f"s_ol{i}") for i in range(RB)]
        s_msg = [sem(f"s_msg{i}") for i in range(9 * NQ)]
        s_gl = [sem(f"s_gl{i}") for i in range(NQ)]
        block = ctx.enter_context(nc.Block())
        general = general_path(nc, x, edges, Ws, bb, vd, out, A8, bank, cst, dg, w, g, lnb, identf, onesf, S, s_msg)

        def ending(eng, name):
            eng.wait_ge(S["s_flag"], 1)
            bad = eng.value_load(flag[0:1, 0:1], min_val=0, max_val=1)
            with eng.If(bad != 0):
                general(eng, name)


        @block.sync
        def _(sp):
            def store(t):
                sp.wait_ge(S["s_o"], t + 1)
                sp.dma_start(out[t * P:t * P + rows(t), :], g[0:rows(t), t % RB, :]).then_inc(s_ol[t % RB], 16)

            sp.dma_start(H[0:BG, :], heads.rearrange("(a n) -> a n", a=1).broadcast_to([BG, N])).then_inc(S["s_h"], 16)
            for c in range(2):
                sp.dma_start(Wraw[:, 4 * c:4 * c + 4, :], Ws[0][:, c * P:(c + 1) * P, :].rearrange("k f n -> f k n"))\
                  .then_inc(S["s_w"], 16)
            for i in range(RB):
                sp.dma_start(xr[:, i, :], x[i * P:(i + 1) * P, :]).then_inc(s_xl[i], 16)
            for L in range(3):
                sp.dma_start(bb[:, L, :], bs[L].rearrange("(a n) -> a n", a=1).broadcast_to([P, F])).then_inc(S["s_b"], 16)
            sp.wait_ge(S["s_dw"], NQ)
            sp.dma_start(degd[0:NG * GW].rearrange("(q p w) -> p q w", q=NQ, w=GW), dgw[:, :, :])\
              .then_inc(S["s_dr"], 16)
            sp.wait_ge(S["s_dr"], 16)
            sp.wait_ge(S["s_dz"], 1)
            sp.dma_start(dgT[0:NT - 1, :], degd[0:(NT - 1) * P].rearrange("(a b) -> a b", b=P)).then_inc(S["s_dt"], 16)
            sp.dma_start(dgT[NT - 1:NT, 0:TAIL], degd[(NT - 1) * P:N].rearrange("(a b) -> a b", a=1))\
              .then_inc(S["s_dt"], 16)
            for i in range(RB, XL):
                if i < NT + RB:
                    sp.wait_ge(S["s_gx"], i - RB + 1)
                elif i < NT + 16 + RB:
                    sp.wait_ge(S["s_wq"], 3 * (i - RB - NT) + 3)
                else:
                    sp.wait_ge(S["s_z"], i - RB - NT - 16 + 1)
                if NT <= i < NT + 16:
                    L, c, k = 1 + (i - NT) // 8, (i - NT) // 4 % 2, (i - NT) % 4
                    sp.dma_start(xr[:, i % RB, :], Ws[L][k, c * P:(c + 1) * P, :]).then_inc(s_xl[i % RB], 16)
                    continue
                t = i if i < NT else i - NT - 16
                sp.dma_start(xr[0:rows(t), i % RB, :], x[t * P:t * P + rows(t), :]).then_inc(s_xl[i % RB], 16)
                if i - NT - 16 - RB >= 0:
                    store(i - NT - 16 - RB)
            for t in range(NT - RB, NT):
                store(t)
            for i in range(RB):
                sp.wait_ge(s_ol[i], 16 * len(range(i, NT, RB)))
            ending(sp, "sp")

        @block.gpsimd
        def _(pool):
            pool.memset(identf[:, :], 0.0).then_inc(S["s_cst"], 1)
            pool.iota(thr[:, 0, :], pattern=[[GW * BG, NQ]], base=0, channel_multiplier=GW,
                      allow_small_or_imprecise_dtypes=True).then_inc(S["s_cst"], 1)
            pool.iota(thr[:, 1, :], pattern=[[GW * BG, NQ]], base=5, channel_multiplier=GW,
                      allow_small_or_imprecise_dtypes=True).then_inc(S["s_cst"], 1)
            pool.iota(thS[:, 0:NQ], pattern=[[2 * GW * BG, NQ]], base=-1, channel_multiplier=2 * GW,
                      allow_small_or_imprecise_dtypes=True).then_inc(S["s_cst"], 1)
            pool.iota(thS[:, NQ:NQ + GW + 1], pattern=[[-2, GW + 1]], base=GW, channel_multiplier=0,
                      allow_small_or_imprecise_dtypes=True).then_inc(S["s_cst"], 1)
            pool.iota(iotaB, pattern=[[1, P], [0, BV]], base=0, channel_multiplier=0,
                      allow_small_or_imprecise_dtypes=True).then_inc(S["s_cst"], 1)
            pool.iota(iotaK[:, :], pattern=[[1, KEYS + 1]], base=-5, channel_multiplier=0,
                      allow_small_or_imprecise_dtypes=True).then_inc(S["s_cst"], 1)
            pool.memset(KBb[:, 2 * NG:2 * NG + BV], -1.0).then_inc(S["s_cst"], 1)
            pool.memset(dgT[:, :], 0.0).then_inc(S["s_dz"], 1)
            pool.memset(want[:, 0:1], float(E)).then_inc(S["s_cst"], 1)
            pool.memset(want[:, 1:2], 0.0).then_inc(S["s_cst"], 1)
            pool.memset(want[:, 2:3], 15.0).then_inc(S["s_cst"], 1)
            pool.memset(onesf[:, :], 1.0).then_inc(S["s_cst"], 1)
            pool.memset(A8[:, :, (NG - 1) * GW:NP], 0.0).then_inc(S["s_cst"], 1)
            pool.wait_ge(S["s_cst"], 1)
            pool.affine_select(out=identf[:, :], in_=identf[:, :], compare_op=ALU.not_equal, fill=1.0, base=0,
                               pattern=[[-1, P]], channel_multiplier=1).then_inc(S["s_cst"], 1)
            for q in range(NQ):
                pool.wait_ge(S["s_idx"], q + 1)
                pool.indirect_dma_start(G[0:BG, q, :, :].rearrange("p s e -> p (s e)"), None, table[:, :],
                                        bass.IndirectOffsetOnAxis(ap=idx[0:BG, q:q + 1], axis=0)).then_inc(s_gl[q], 16)
            pool.wait_ge(S["s_w"], 32)
            hl = Whl[:, 0].rearrange("p c k n -> p (c k) n")
            pool.tensor_scalar(Wsc, Wraw, SV * SC, None, ALU.mult).then_inc(S["s_wp"], 1)
            pool.wait_ge(S["s_whi"], 1)
            pool.wait_ge(S["s_wp"], 1)
            pool.tensor_scalar(Wraw, hl[:, :, 0:F], SC, None, ALU.mult).then_inc(S["s_wp"], 1)
            pool.wait_ge(S["s_wp"], 2)
            pool.tensor_tensor(hl[:, :, F:512], Wsc, Wraw, ALU.subtract).then_inc(S["s_wp"], 1)
            pool.wait_ge(S["s_cs"], 1)
            for t in range(NT):
                pool.wait_ge(s_xl[t % RB], 16 * (t // RB + 1))
                if t >= RB:
                    pool.wait_ge(S["s_tp"], t - RB + 1)
                pool.tensor_scalar(g[:, t % RB, :], xr[:, t % RB, :], cst[:, 2, t:t + 1], 0.0, ALU.mult,
                                   ALU.add).then_inc(S["s_gx"], 1)
            for t in range(NT):
                pool.wait_ge(S["s_ev"], groups_of(t)[-1] + 1)
                src = A8[0:HALF, NT - 1, t * P:(t + 1) * P]
                pool.tensor_copy(AT[0:HALF, t * P:(t + 1) * P], src).then_inc(S["s_at"], 1)
                pool.wait_ge(S["s_at"], 2 * t + 1)
                pool.tensor_scalar(AT[HALF:P, t * P:(t + 1) * P], AT[0:HALF, t * P:(t + 1) * P], 1.0 / SC, 0.0, ALU.mult,
                                   ALU.add).then_inc(S["s_at"], 1)
            for i in range(16):
                L, c, k = 1 + i // 8, i // 4 % 2, i % 4
                raw = xr[:, (NT + i) % RB, :]
                pool.wait_ge(S["s_wi"], i + 1)
                pool.tensor_scalar(raw, raw, SV, 0.0, ALU.mult, ALU.add).then_inc(S["s_wq"], 1)
                pool.wait_ge(S["s_wq"], 3 * i + 1)
                pool.tensor_tensor(raw, raw, Whl[:, L, c, k, 0:F], ALU.subtract).then_inc(S["s_wq"], 1)
                pool.wait_ge(S["s_wq"], 3 * i + 2)
                pool.tensor_scalar(Whl[:, L, c, k, F:512], raw, SC, 0.0, ALU.mult, ALU.add).then_inc(S["s_wq"], 1)
            ending(pool, "pool")

        @block.scalar
        def _(act):
            act.wait_ge(S["s_h"], 16)
            act.wait_ge(S["s_cst"], 5)
            for q in range(1, NQ):
                act.activation(V[0][0:BG, 7 * (q - 1):7 * q, :].rearrange("p a b -> p (a b)")[:, 0:N], H16[0:BG, :],
                               ACT.Sign, scale=-2.0, bias=thS[0:BG, q:q + 1],
                               accum_out=cS[0:BG, q:q + 1]).then_inc(S["s_sg"], 1)
            act.wait_ge(S["s_dl"], 1)
            for i in range(GW + 1):
                act.activation(V[0][0:BG, 14, 0:256] if i == 0 else V[0][0:BG, 14 + i // 2, 256 * (i % 2):][:, 0:256],
                               g[0:BG, 0, :], ACT.Sign, scale=2.0, bias=thS[0:BG, NQ + i:NQ + i + 1],
                               accum_out=cS[0:BG, NQ + i:NQ + i + 1]).then_inc(S["s_sg"], 1)
            act.wait_ge(S["s_w"], 32)
            act.activation(Whl[:, 0].rearrange("p c k n -> p (c k) n")[:, :, 0:F], Wraw, ACT.Copy,
                           scale=SV).then_inc(S["s_whi"], 1)
            act.wait_ge(S["s_cst"], 14)

            def columns(gi):
                n = min(GW, N - gi * GW)
                act.wait_ge(S["s_vis"], gi + 1)
                act.activation(A8[:, :, gi * GW:gi * GW + n],
                               BB[gi % 2][:, 0:KEYS].rearrange("p (a w) -> p a w", w=GW)[:, :, 0:n],
                               ACT.Copy, saturate=False).then_inc(S["s_ev"], 1)

            for gi in groups_of(0):
                columns(gi)
            act.wait_ge(S["s_dg"], 2)
            act.activation(dg[:, 2, :], dg[:, 1, :], ACT.Sqrt).then_inc(S["s_sq"], 1)
            act.wait_ge(S["s_cs"], 1)
            for it in trailing(SCHED, 1, 4):
                if it[0] == "B":
                    columns(it[1])
                    continue
                if it[0] == "T":
                    _, L, t = it
                    j = t_no[(L, t)]
                    act.wait_ge(S["s_tp"], j + 1)
                    act.activation(gT[:, t, :, 0, :], TB[j % 2][:, 0:F].rearrange("p (c m) -> p c m", c=2),
                                   ACT.Copy, scale=1.0 / SC).then_inc(S["s_th"], 1)
                    continue
                what, L, k, t = it
                e = pe_no[(L, k, t)]
                if what == "V":
                    v = v_no[(L, k, t)]
                    act.wait_ge(S["s_d1"], e + 1)
                    r = P if t < NT - 1 else HALF
                    act.activation(V[vbuf[(L, k)]][0:r, t, 0:F], PB[e][0:r, 0:F], ACT.Copy,
                                   scale=1.0 / SC).then_inc(S["s_a2"], 1)
                    if (L, k) == (0, 1) and t < 16:
                        i = NT + t
                        act.wait_ge(s_xl[i % RB], 16 * (i // RB + 1))
                        act.wait_ge(S["s_vis"], NG)
                        act.activation(Whl[:, 1 + t // 8, t // 4 % 2, t % 4, 0:F], xr[:, i % RB, :], ACT.Copy,
                                       scale=SV).then_inc(S["s_wi"], 1)
                    continue
                act.wait_ge(S["s_ps"], e + 1)
                if e >= RB:
                    act.wait_ge(S["s_d1"], e - RB + 1)
                lo = PB[e][:, F:512]
                if k > 0:
                    sc = cst[:, 0, t:t + 1]
                elif L < 2:
                    sc = 1.0 / SV
                else:
                    sc = cst[:, 4, t:t + 1]
                act.activation(t1[:, e % RB, :], lo, ACT.Copy, scale=sc).then_inc(S["s_a1"], 1)
                if k == 0 and L == 2:
                    act.wait_ge(S["s_ln"], t + 1)
                    act.activation(lnb[:, t % RB, 8:9], lnb[:, t % RB, 7:8], ACT.Sqrt).then_inc(S["s_sd"], 1)
            ending(act, "act")

        @block.tensor
        def _(pe):
            pe.wait_ge(S["s_cst"], 14)

            def emptied(was):
                if was[1] > 0:
                    pe.wait_ge(S["s_v"], v_no[was] + 1)
                else:
                    pe.wait_ge(S["s_d1"], pe_no[was] + 1)

            def build(gi):
                if gi == len(groups_of(0)):
                    emptied(p_of[last_init])
                if gi >= 2:
                    pe.wait_ge(S["s_ev"], gi - 1)
                pe.wait_ge(S["s_ob"], 2 * gi // BV + 1)
                for k in range(2):
                    vis = 2 * gi + k
                    pe.wait_ge(S["s_oh"], vis + 1)
                    mm = pe.matmul(BB[gi % 2][:, 0:KEYS], OB[:, vis // BV % NO, :, vis % BV],
                                   OK[:, vis % NR, 0:KEYS], start=(k == 0), stop=(k == 1))
                mm.then_inc(S["s_vis"], 1)

            for q in range(NQ):
                pe.wait_ge(S["s_ki"], q + 1)
                if q:
                    pe.wait_ge(S["s_kb"], 2 * q)
                for m in range(4):
                    src = tmf[0:BG, 2 + m // 2, (m % 2) * P:(m % 2 + 1) * P]
                    mm = pe.transpose(bank[7][:, m * P:m * P + BG], src, identf[0:BG, 0:BG])
                mm.then_inc(S["s_kt"], 1)
            for gi in groups_of(0):
                build(gi)
            pe.wait_ge(S["s_dt"], 32)
            pe.transpose(bank[7][:, 0:NT], dgT[:, :], identf[0:NT, 0:NT]).then_inc(S["s_deg"], 1)
            pe.wait_ge(S["s_wp"], 3)
            for it in SCHED:
                if it[0] == "T":
                    _, L, t = it
                    j = t_no[(L, t)]
                    if L == 0:
                        pe.wait_ge(S["s_gx"], t + 1)
                    else:
                        pe.wait_ge(S["s_g"], j - NT + 1)
                    if j >= 2:
                        pe.wait_ge(S["s_tl"], j - 1)
                    for c in range(2):
                        mm = pe.transpose(TB[j % 2][:, c * P:(c + 1) * P], g[:, j % RB, c * P:(c + 1) * P],
                                          identf[:, :])
                    mm.then_inc(S["s_tp"], 1)
                    continue
                _, L, k, t = it
                e = pe_no[(L, k, t)]
                if e in user:
                    emptied(p_of[user[e]])
                elif bank_of[e] > 4:
                    pe.wait_ge(S["s_ev"], len(groups_of(0)))
                if (L, k, t) == (0, 1, 0):
                    pe.wait_ge(S["s_ev"], NG)
                if (L, k, t) == (1, 3, 0):
                    pe.wait_ge(S["s_wq"], 48)
                if k == 3:
                    pe.wait_ge(S["s_tl"], t_no[(L, t)] + 1)
                acc = PB[e]
                for c in range(2):
                    pe.matmul(acc[:, :], gT[:, t, c, 0, :], Whl[:, L, c, k, :], start=(c == 0), stop=False,
                              skip_group_check=True)
                    mm = pe.matmul(acc[:, F:512], gT[:, t, c, 1, :], Whl[:, L, c, k, 0:F], start=False,
                                   stop=(k == 3 and c == 1), skip_group_check=True)
                if k < 3:
                    src = V[vbuf[(L, k + 1)]]
                    coming = groups_of(t + 1) if (L, k) == (0, 2) else []
                    if (L, k) == (0, 2):
                        pe.wait_ge(S["s_ev"], groups_of(t)[-1] + 1)
                    for a in range(NT):
                        if a % 2 == 0 and a // 2 < len(coming):
                            build(coming[a // 2])
                        if t == 0:
                            pe.wait_ge(S["s_v"], v_no[(L, k + 1, a)] + 1)
                        if a < NT - 1:
                            mm = pe.matmul(acc[:, :], A8[:, a, t * P:(t + 1) * P], src[:, a, :], start=False,
                                           stop=False, skip_group_check=True)
                            continue
                        if (L, k) == (0, 2):
                            pe.wait_ge(S["s_at"], 2 * t + 2)
                        mm = pe.matmul(acc[:, 0:F], AT[:, t * P:(t + 1) * P], src[:, a, 0:F], start=False,
                                       stop=True, skip_group_check=True)
                mm.then_inc(S["s_ps"], 1)
                if (L, k, t) == (2, 0, 13):
                    pe.wait_ge(S["s_ck"], 1)
                    pe.transpose(bank[7][0:15, 0:P], chk[:, 0:15], identf[:, :]).then_inc(S["s_pk"], 1)
                if (L, k, t) == (2, 0, 18):
                    pe.wait_ge(S["s_ck"], 2)
                    pe.matmul(bank[7][0:1, 128:130], onesf[:, 0:1], chk[:, 15:17], start=True, stop=True)
                    pe.matmul(bank[7][0:1, 130:131], onesf[0:15, 0:1], chk[0:15, 21:22], start=True,
                              stop=True).then_inc(S["s_pk"], 1)
            ending(pe, "pe")

        @block.vector
        def _(dve):
            dve.wait_ge(S["s_h"], 16)
            dve.wait_ge(S["s_cst"], 3)
            dve.tensor_scalar(junk[0:BG, :], H16[0:BG, :], thr[0:BG, 0, 0:1], None, ALU.is_lt, ALU.add,
                              accum_out=cnt[0:BG, 0:1]).then_inc(S["s_cnt"], 1)
            dve.wait_ge(S["s_cnt"], 1)
            dve.tensor_scalar(idx[0:BG, 0:1], cnt[0:BG, 0:1], -1.0, 0.0, ALU.add, ALU.max).then_inc(S["s_idx"], 1)
            for q in range(1, NQ):
                dve.wait_ge(S["s_sg"], q)
                dve.tensor_scalar(cnt[0:BG, q:q + 1], cS[0:BG, q:q + 1], float(N - 2), 0.0, ALU.add,
                                  ALU.max).then_inc(S["s_cnt"], 1)
                dve.wait_ge(S["s_cnt"], q + 1)
                dve.tensor_scalar(idx[0:BG, q:q + 1], cnt[0:BG, q:q + 1], 0.5, None, ALU.mult).then_inc(S["s_idx"], 1)
            kk = 0

            def link(ins):
                nonlocal kk
                kk += 1
                ins.then_inc(S["s_wk"], 1)
                dve.wait_ge(S["s_wk"], kk)

            dve.wait_ge(S["s_cst"], 14)
            for q in range(NQ):
                dve.wait_ge(s_gl[q], 16)
                s_, d_ = G[0:BG, q, 0, :], G[0:BG, q, 1, :]
                ai = w[0:BG, 0, :].bitcast(I32)
                bi = w[0:BG, 1, :].bitcast(I32)
                dl, sq = g[0:BG, 0, :] if q == 0 else w[0:BG, 2, :], w[0:BG, 3, :]
                if q:
                    dve.wait_ge(S["s_kt"], q)
                link(dve.tensor_scalar(ai, s_, 7, None, ALU.logical_shift_right))
                link(dve.tensor_scalar(bi, s_, P - 1, None, ALU.bitwise_and))
                link(dve.tensor_copy(t1[0:BG, 3, :], bi))
                link(dve.tensor_scalar(dl, d_, thr[0:BG, 1, q:q + 1], None, ALU.subtract))
                if q == 0:
                    dve.sem_inc(S["s_dl"], 1)
                link(dve.tensor_tensor(sq, dl, dl, ALU.mult))
                link(dve.tensor_scalar(t1[0:BG, 0, :], sq, 25.5, FAR, ALU.is_gt, ALU.mult))
                link(dve.scalar_tensor_tensor(t1[0:BG, 1, :], ai, float(GW), dl, ALU.mult, ALU.add))
                dve.tensor_tensor(t1[0:BG, 2, :], t1[0:BG, 0, :], t1[0:BG, 1, :], ALU.add).then_inc(S["s_ki"], 1)
                if q > 1:
                    dve.wait_ge(S["s_dw"], q - 1)
                for i in range(GW if q else 0):
                    last = dve.tensor_scalar(junk[0:BG, i * WIN:(i + 1) * WIN], dl, float(i - 5), None,
                                             ALU.is_equal, ALU.add, accum_out=dgw[:, q, i:i + 1])
                if q:
                    last.then_inc(S["s_dw"], 1)
                dve.wait_ge(S["s_kt"], q + 1)
                kt = bank[7][:, :].rearrange("p (m e) -> p m e", m=4)
                dve.tensor_copy(KBk[:, 2 * BG * q:2 * BG * (q + 1)].rearrange("p (e k) -> p k e", k=2),
                                kt[:, 0:2, 0:BG]).then_inc(S["s_kb"], 1)
                dve.tensor_copy(KBb[:, 2 * BG * q:2 * BG * (q + 1)].rearrange("p (e k) -> p k e", k=2),
                                kt[:, 2:4, 0:BG]).then_inc(S["s_kb"], 1)

            dve.wait_ge(S["s_sg"], NQ + GW)
            link(dve.tensor_tensor(cS[0:BG, 0:GW], cS[0:BG, NQ:NQ + GW], cS[0:BG, NQ + 1:NQ + GW + 1], ALU.subtract))
            dve.tensor_scalar(dgw[:, 0, :], cS[0:BG, 0:GW], 0.5, None, ALU.mult).then_inc(S["s_dw"], 1)

            def onehots(gi):
                if 2 * gi % BV == 0:
                    i = 2 * gi // BV
                    if i == 0:
                        dve.wait_ge(S["s_kb"], 2 * NQ)
                    if i >= NO:
                        dve.wait_ge(S["s_vis"], (i - NO + 1) * BV // 2)
                    dve.tensor_tensor(OB[:, i % NO, :, :], iotaB,
                                      KBb[:, BV * i:BV * (i + 1)].unsqueeze(1).broadcast_to([P, P, BV]),
                                      ALU.is_equal).then_inc(S["s_ob"], 1)
                for k in range(2):
                    vis = 2 * gi + k
                    if vis >= NR:
                        dve.wait_ge(S["s_vis"], (vis - NR) // 2 + 1)
                    dve.tensor_scalar(OK[:, vis % NR, 0:KEYS], iotaK[:, 0:KEYS], KBk[:, vis:vis + 1], None,
                                      ALU.is_equal).then_inc(S["s_oh"], 1)

            for gi in groups_of(0):
                onehots(gi)
            nd = 0

            def dl_(ins):
                nonlocal nd
                nd += 1
                ins.then_inc(S["s_dd"], 1)
                dve.wait_ge(S["s_dd"], nd)

            dve.wait_ge(S["s_deg"], 1)
            dve.tensor_copy(dg[:, 0, :], bank[7][:, 0:NT]).then_inc(S["s_dg"], 1)
            dve.wait_ge(S["s_dg"], 1)
            dve.tensor_scalar(dg[:, 1, :], dg[:, 0, :], 1.0, None, ALU.max).then_inc(S["s_dg"], 1)
            dve.wait_ge(S["s_dg"], 2)
            dl_(dve.reciprocal(dg[:, 3, :], dg[:, 1, :]))
            dl_(dve.tensor_scalar(dg[:, 4, :], dg[:, 0, :], 1.0, None, ALU.min))
            dl_(dve.tensor_tensor(cst[:, 0, :], dg[:, 3, :], dg[:, 4, :], ALU.mult))
            dl_(dve.tensor_scalar(cst[:, 1, :], cst[:, 0, :], SC, None, ALU.mult))
            dve.wait_ge(S["s_sq"], 1)
            dl_(dve.reciprocal(dg[:, 5, :], dg[:, 2, :]))
            dl_(dve.tensor_tensor(dg[:, 6, :], dg[:, 5, :], dg[:, 1, :], ALU.mult))
            dl_(dve.tensor_tensor(dg[:, 7, :], dg[:, 6, :], dg[:, 2, :], ALU.add))
            dl_(dve.tensor_scalar(cst[:, 2, :], dg[:, 7, :], 0.5 * SC, None, ALU.mult))
            dl_(dve.reciprocal(dg[:, 5, :], dg[:, 7, :]))
            dl_(dve.tensor_scalar(cst[:, 3, :], dg[:, 5, :], 2.0 / SV, None, ALU.mult))
            dve.tensor_scalar(cst[:, 4, :], dg[:, 5, :], 2.0 / (SV * SC), None, ALU.mult).then_inc(S["s_cs"], 1)
            dve.wait_ge(S["s_cs"], 1)
            dve.wait_ge(S["s_b"], 48)
            nst = nam = 0

            def largest(col, ap, axis):
                nonlocal nst
                dve.tensor_reduce(stat[:, col:col + 1], ap, axis, ALU.max,
                                  apply_absolute_value=True).then_inc(S["s_st"], 1)
                nst += 1

            def verdict(part):
                if part == 0:
                    verdict_maxima()
                elif part == 1:
                    verdict_ranges()
                else:
                    dve.wait_ge(S["s_pk"], 2)
                    dl_(dve.tensor_copy(chk[0:1, 24:27], bank[7][0:1, 128:131]))
                    dl_(dve.tensor_tensor(chk[0:1, 28:31], chk[0:1, 24:27], want[:, 0:3], ALU.not_equal))
                    dve.tensor_reduce(flag[:, 0:1], chk[0:1, 28:31], AX.X, ALU.max).then_inc(S["s_flag"], 1)

            def verdict_maxima():
                assert nam == NAM
                dve.wait_ge(S["s_st"], nst)
                dl_(dve.tensor_reduce(chk[:, 0:12], stat[:, 0:12 * NT].rearrange("p (m t) -> p m t", t=NT), AX.X,
                                      ALU.max))
                dl_(dve.tensor_copy(chk[:, 12:15], stat[:, 12 * NT:12 * NT + 3]))
                dl_(dve.tensor_reduce(chk[:, 15:16], dg[:, 0, :], AX.X, ALU.add))
                dl_(dve.tensor_reduce(chk[:, 17:18], ast[:, :], AX.X, ALU.max))
                dve.tensor_scalar(chk[:, 16:17], chk[:, 17:18], AMAX, None, ALU.is_ge).then_inc(S["s_ck"], 1)

            def verdict_ranges():
                dve.wait_ge(S["s_pk"], 1)
                dl_(dve.tensor_reduce(chk[0:15, 18:19], bank[7][0:15, 0:P], AX.X, ALU.max))
                dl_(dve.tensor_scalar(chk[0:15, 19:20], chk[0:15, 18:19], LOW, None, ALU.is_ge))
                dl_(dve.tensor_scalar(chk[0:15, 20:21], chk[0:15, 18:19], HIGH, None, ALU.is_le))
                dve.tensor_tensor(chk[0:15, 21:22], chk[0:15, 19:20], chk[0:15, 20:21],
                                  ALU.mult).then_inc(S["s_ck"], 1)

            for it in trailing(SCHED, 7, 9):
                if it[0] == "B":
                    onehots(it[1])
                    continue
                if it[0] == "T":
                    _, L, t = it
                    j = t_no[(L, t)]
                    dve.wait_ge(S["s_th"], j + 1)
                    dve.scalar_tensor_tensor(gT[:, t, :, 1, :], gT[:, t, :, 0, :], -SC,
                                             TB[j % 2][:, 0:F].rearrange("p (c m) -> p c m", c=2),
                                             ALU.mult, ALU.add).then_inc(S["s_tl"], 1)
                    if L:
                        largest(9 * NT + j, gT[:, t, :, 0, :], AX.XY)
                    continue
                what, L, k, t = it
                e = pe_no[(L, k, t)]
                hi = PB[e][:, 0:F]
                we = w[:, t % 2, :]
                if k > 0:
                    v = v_no[(L, k, t)]
                    vb = V[vbuf[(L, k)]]
                if what == "V":
                    dve.wait_ge(S["s_a2"], v + 1)
                    if t < NT - 1:
                        lo, r = vb[:, t, F:512], P
                    else:
                        lo, r = vb[HALF:P, t, 0:F], HALF
                    dve.scalar_tensor_tensor(lo, vb[0:r, t, 0:F], -SC, hi[0:r, :], ALU.mult,
                                             ALU.add).then_inc(S["s_v"], 1)
                    if (L, k) not in ((0, 3), (0, 2)):
                        if t == NT - 1:
                            dve.wait_ge(S["s_v"], v + 1)
                        largest(v, vb[:, t, 0:F], AX.X)
                    if (L, k) == (0, 1):
                        largest(9 * NT + t, gT[:, t, :, 0, :], AX.XY)
                        largest(v_no[(0, 2, t)], V[vbuf[(0, 2)]][:, t, 0:F], AX.X)
                    if (L, k) == (1, 1) and t < 3:
                        largest(12 * NT + t, Whl[:, t].rearrange("p c k n -> p (c k) n")[:, :, 0:F], AX.XY)
                    if k < 3 and L > 0 and nam < NAM:
                        a_, i_ = nam // 4, nam % 4
                        dve.tensor_reduce(ast[:, nam:nam + 1], A8[:, a_, 800 * i_:800 * i_ + 800].bitcast(U8), AX.X,
                                          ALU.max).then_inc(S["s_st"], 1)
                        nam += 1
                        nst += 1
                    continue
                if k > 0:
                    if (L, k) == (0, 1):
                        largest(v_no[(0, 3, t)], vb[:, t, 0:F], AX.X)
                    dve.wait_ge(S["s_a1"], e + 1)
                    dve.scalar_tensor_tensor(hi, hi, cst[:, 1, t:t + 1], t1[:, e % RB, :], ALU.mult,
                                             ALU.add).then_inc(S["s_d1"], 1)
                elif L < 2:
                    j = t_no[(L + 1, t)]
                    dve.wait_ge(S["s_a1"], e + 1)
                    dl_(dve.scalar_tensor_tensor(t2[:, t % 2, :], bb[:, L, :], cst[:, 2, t:t + 1],
                                                 t1[:, e % RB, :], ALU.mult, ALU.add))
                    dve.scalar_tensor_tensor(we, hi, SC / SV, t2[:, t % 2, :], ALU.mult,
                                             ALU.add).then_inc(S["s_d1"], 1)
                    dve.wait_ge(S["s_d1"], e + 1)
                    dve.wait_ge(S["s_tp"], j - RB + 1)
                    dve.tensor_scalar(g[:, j % RB, :], we, 0.0, None, ALU.max).then_inc(S["s_g"], 1)
                else:
                    i = NT + 16 + t
                    if t in (10, 15, 20):
                        verdict((t - 10) // 5)
                    dve.wait_ge(s_xl[i % RB], 16 * (i // RB + 1))
                    r = rows(t)
                    dve.tensor_tensor(t2[:, t % 2, :], xr[:, i % RB, :], bb[:, 2, :], ALU.add).then_inc(S["s_z"], 1)
                    dve.wait_ge(S["s_a1"], e + 1)
                    dve.scalar_tensor_tensor(we, hi, cst[:, 3, t:t + 1], t1[:, e % RB, :], ALU.mult,
                                             ALU.add).then_inc(S["s_d1"], 1)
                    dve.wait_ge(S["s_d1"], e + 1)
                    dve.wait_ge(S["s_z"], t + 1)
                    dl_(dve.tensor_tensor(we, we, t2[:, t % 2, :], ALU.add))
                    ln = lnb[:, t % RB, :]
                    dl_(dve.bn_stats(ln[:, 0:6], we))
                    dl_(dve.bn_aggr(ln[:, 6:8], ln[:, 0:6]))
                    dve.tensor_scalar(ln[:, 7:8], ln[:, 7:8], EPS, None, ALU.add).then_inc(S["s_ln"], 1)
                    dve.wait_ge(S["s_sd"], t + 1)
                    dl_(dve.reciprocal(ln[:, 9:10], ln[:, 8:9]))
                    dl_(dve.scalar_tensor_tensor(ln[:, 10:11], ln[:, 9:10], ln[:, 7:8], ln[:, 8:9], ALU.mult, ALU.add))
                    dl_(dve.reciprocal(ln[:, 11:12], ln[:, 10:11]))
                    dl_(dve.tensor_scalar(ln[:, 9:10], ln[:, 11:12], 2.0, None, ALU.mult))
                    if t >= RB:
                        dve.wait_ge(s_ol[t % RB], 16 * (t // RB))
                    dve.tensor_scalar(g[:, t % RB, :], we, ln[:, 6:7], ln[:, 9:10], ALU.subtract,
                                      ALU.mult).then_inc(S["s_o"], 1)
            ending(dve, "dve")


def kernel(**inputs):
    import numpy as _np
    import concourse.bacc as _bacc
    from concourse import mybir as _mybir
    from concourse.bass_utils import run_bass_kernel_spmd as _run

    nc = _bacc.Bacc("TRN2", target_bir_lowering=False, num_devices=1)
    src = _np.asarray(inputs["src"])
    dst = _np.asarray(inputs["dst"])
    pad = _np.full(WIN, -1, _np.int32)
    srcp = _np.concatenate([src, pad])
    dstp = _np.concatenate([dst, pad])
    at = _np.arange(0, E, GRAN)[:, None] + _np.arange(WIN)[None, :]
    arrays = {"x": _np.ascontiguousarray(inputs["x"]),
              "table": _np.ascontiguousarray(_np.concatenate([srcp[at], dstp[at]], axis=1)),
              "edges": _np.ascontiguousarray(_np.stack([_np.concatenate([src, _np.zeros(NCH * P - E, _np.int32)]),
                                                        dstp[:NCH * P]]).reshape(2, P, NCH)),
              "heads": _np.ascontiguousarray(dst[::GRAN])}
    for i in (1, 2, 3):
        arrays[f"W{i}"] = _np.ascontiguousarray(inputs[f"L0_gnn_W{i}"])
        arrays[f"b{i}"] = _np.ascontiguousarray(inputs[f"L0_gnn_b{i}"])
    ap = {k: nc.dram_tensor("in_" + k, v.shape, _mybir.dt.from_np(v.dtype), kind="ExternalInput").ap()
          for k, v in arrays.items()}
    out = nc.dram_tensor("out_0", (N, F), _mybir.dt.float32, kind="ExternalOutput").ap()
    degd = nc.dram_tensor("degd", (NG * GW,), _mybir.dt.float32, kind="Internal").ap()
    vd = [nc.dram_tensor(f"vd{i}", (NP, F), _mybir.dt.float32, kind="Internal").ap() for i in range(2)]
    bass_tag_gnn_layernorm(nc, ap["x"], ap["table"], ap["heads"], ap["edges"], [ap["W1"], ap["W2"], ap["W3"]],
                           [ap["b1"], ap["b2"], ap["b3"]], vd, degd, out)
    r = _run(nc, [{"in_" + k: v for k, v in arrays.items()}], core_ids=[0])
    return r.results[0]["out_0"]
```

```python
from contextlib import ExitStack

import concourse.bass as bass
from concourse import mybir

P = 128
N = 3125
E = 50000
F = 256
NT = 25
NP = NT * P
TAIL = N - (NT - 1) * P
GD = 4
GS = 5
GW = GS * GD
NW = -(-N // GD)
NG = -(-NW // GS)
NQ = 3
QW = 7
JW = QW * P
HP = 125
HN = N // HP
CHUNK = ((0, 2), (2, 4), (4, 7))
KEYS = NT * GD
WIN = 128
GRAN = 16
BV = 8
NB = -(-NW // BV)
NO = 3
CST = 14
WQ, WT, WP = 3, 10, 15
AHEAD = 4
AQ = (0, 1, 2, 3)
AL = (3, 8, 12, 16, 20, 23)
FAR = 10000.0
RB = 4
SC = 2048.0
SV = 16.0
EPS = 1e-5
HALF = 64
XL = 2 * NT + 16
NCH = -(-E // P)
PT = 9
LOW = 2.0 ** -10
HIGH = 60000.0
AMAX = 87.5
NAM = 4 * NT

ALU = mybir.AluOpType
ACT = mybir.ActivationFunctionType
AX = mybir.AxisListType
F32 = mybir.dt.float32
F16 = mybir.dt.float16
F8 = mybir.dt.float8e4
I32 = mybir.dt.int32
U8 = mybir.dt.uint8


def rows(t):
    return P if t < NT - 1 else TAIL


def schedule():
    out = [("T", 0, 0), ("T", 0, 1)]
    for t in range(NT):
        if t + 2 < NT:
            out.append(("T", 0, t + 2))
        out.append(("P", 0, 3, t))
    for L in range(3):
        for k in (2, 1, 0):
            for t in range(NT):
                out.append(("P", L, k, t))
                if k == 0 and L < 2:
                    if t >= 1:
                        out.append(("T", L + 1, t - 1))
                    if t >= 2:
                        out.append(("P", L + 1, 3, t - 2))
        if L < 2:
            out.append(("P", L + 1, 3, NT - 2))
            out.append(("T", L + 1, NT - 1))
            out.append(("P", L + 1, 3, NT - 1))
    return out


def general_path(nc, x, edges, Ws, bb, vd, out, A8, bank, cst, dg, w, g, lnb, identf, onesf, S, s_msg):
    line = []
    region = A8[:, :, :].rearrange("p a b -> p (a b)")
    at = [0]

    def take(n, dt=F32):
        v = region[:, at[0]:at[0] + 4 * n].bitcast(dt)
        at[0] += 4 * n
        return v

    gTs = take(2 * NP).rearrange("p (c n) -> p c n", c=2)
    Wf = take(2048).rearrange("p (c k n) -> p c k n", c=2, k=4)
    iot = take(PT * P)
    oh = take(PT * P)
    msg = take(F)
    srcI = take(NCH, I32)
    dstI = take(NCH, I32)
    dstF = take(NCH)
    tmI = take(NCH, I32)
    dhi = take(NCH)
    dlo = take(NCH)
    sm = take(16)
    smi = take(4, I32)

    def op(name, fn, inc=1):
        line.append((name, fn, inc))

    def loop(fns, lp):
        line.append(("loop", fns, lp))

    def opened(e):
        e.sem_inc(S["s_ld"], 1)
        e.sem_inc(S["s_turn"], 1)

    op("sp", opened, 0)
    op("sp", lambda e: e.dma_start(srcI, edges[0, :, :]), 16)
    op("sp", lambda e: e.dma_start(dstI, edges[1, :, :]), 16)
    op("pool", lambda e: e.iota(iot, pattern=[[1, PT * P]], base=0, channel_multiplier=0,
                                allow_small_or_imprecise_dtypes=True))
    op("dve", lambda e: e.tensor_copy(dstF, dstI))
    op("dve", lambda e: e.tensor_scalar(tmI, dstI, 7, None, ALU.logical_shift_right))
    op("dve", lambda e: e.tensor_copy(dhi, tmI))
    op("dve", lambda e: e.tensor_scalar(tmI, dstI, P - 1, None, ALU.bitwise_and))
    op("dve", lambda e: e.tensor_copy(dlo, tmI))
    op("dve", lambda e: e.memset(oh, 0.0))
    DG = bank[7]
    op("pe", lambda e: e.matmul(DG[:, 0:NT], oh[:, 0:P], oh[:, 0:NT], start=True, stop=False, skip_group_check=True))
    loops = [0]

    def deg_dve(e, i, n0):
        e.wait_ge(S["s_ld"], i + n0 + 1)
        e.tensor_scalar(oh[:, 0:P], iot[:, 0:P], dlo[:, bass.ds(i, 1)], None, ALU.is_equal)
        e.tensor_scalar(oh[:, P:P + NT], iot[:, 0:NT], dhi[:, bass.ds(i, 1)], None,
                        ALU.is_equal).then_inc(S["s_lp"], 1)

    def deg_pe(e, i, n0):
        e.wait_ge(S["s_lp"], i + n0 + 1)
        e.matmul(DG[:, 0:NT], oh[:, 0:P], oh[:, P:P + NT], start=False, stop=False,
                 skip_group_check=True).then_inc(S["s_ld"], 1)

    loop({"dve": deg_dve, "pe": deg_pe}, 0)
    op("dve", lambda e: e.tensor_copy(dg[:, 0, :], DG[:, 0:NT]))
    op("dve", lambda e: e.tensor_scalar(dg[:, 1, :], dg[:, 0, :], 1.0, None, ALU.max))
    op("act", lambda e: e.activation(dg[:, 2, :], dg[:, 1, :], ACT.Sqrt))
    op("dve", lambda e: e.reciprocal(dg[:, 3, :], dg[:, 1, :]))
    op("dve", lambda e: e.tensor_scalar(dg[:, 4, :], dg[:, 0, :], 1.0, None, ALU.min))
    op("dve", lambda e: e.tensor_tensor(cst[:, 0, :], dg[:, 3, :], dg[:, 4, :], ALU.mult))
    op("dve", lambda e: e.reciprocal(dg[:, 5, :], dg[:, 2, :]))
    op("dve", lambda e: e.tensor_tensor(dg[:, 6, :], dg[:, 5, :], dg[:, 1, :], ALU.mult))
    op("dve", lambda e: e.tensor_tensor(dg[:, 7, :], dg[:, 6, :], dg[:, 2, :], ALU.add))
    op("dve", lambda e: e.tensor_scalar(cst[:, 2, :], dg[:, 7, :], 0.5, None, ALU.mult))
    op("dve", lambda e: e.reciprocal(cst[:, 3, :], cst[:, 2, :]))
    wt, wu = w[:, 0, :], w[:, 1, :]
    gt, xt = g[:, 0, :], g[:, 1, :]

    def turned(t):
        for c in range(2):
            op("pe", lambda e, c=c: e.transpose(bank[6][:, c * P:(c + 1) * P], gt[:, c * P:(c + 1) * P],
                                                identf[:, :]))
        op("dve", lambda e: e.tensor_copy(gTs[:, :, t * P:(t + 1) * P],
                                          bank[6][:, 0:F].rearrange("p (c m) -> p c m", c=2)))

    def project(L, k, t, acc, first):
        for c in range(2):
            op("pe", lambda e, c=c: e.matmul(acc, gTs[:, c, t * P:(t + 1) * P], Wf[:, c, k, :],
                                             start=(first and c == 0), stop=False, skip_group_check=True))

    def v_out(t, acc, b):
        op("dve", lambda e: e.tensor_scalar(wt, acc, cst[:, 0, t:t + 1], None, ALU.mult))
        op("sp", lambda e: e.dma_start(vd[b][t * P:(t + 1) * P, :], wt), 16)

    op("dve", lambda e: e.memset(xt, 0.0))
    for t in range(NT):
        op("sp", lambda e, t=t: e.dma_start(xt[0:rows(t), :], x[t * P:t * P + rows(t), :]), 16)
        op("dve", lambda e, t=t: e.tensor_scalar(gt, xt, cst[:, 2, t:t + 1], None, ALU.mult))
        turned(t)
    for L in range(3):
        for c in range(2):
            op("sp", lambda e, L=L, c=c: e.dma_start(
                Wf[:, c, :, :], Ws[L][:, c * P:(c + 1) * P, :].rearrange("k f n -> f k n")), 16)
        for t in range(NT):
            acc = bank[0][:, 0:F]
            project(L, 3, t, acc, True)
            v_out(t, acc, 1)
        for k in (2, 1, 0):
            for q in range(NQ):
                tiles = list(range(q * PT, min(NT, (q + 1) * PT)))
                accs = {t: bank[(t - q * PT) // 2][:, F * ((t - q * PT) % 2):F * ((t - q * PT) % 2) + F]
                        for t in tiles}
                for t in tiles:
                    project(L, k, t, accs[t], (t - q * PT) % 2 == 0)
                loops[0] += 1

                def hop_dve(e, i, n0, q=q):
                    e.wait_ge(S["s_ld"], i + n0 + 1)
                    e.tensor_copy(smi[:, 0:1], srcI[:, bass.ds(i, 1)])
                    e.tensor_scalar(sm[:, 0:1], dstF[:, bass.ds(i, 1)], float(-q * PT * P), None,
                                    ALU.add).then_inc(S["s_lp"], 1)
                    e.wait_ge(S["s_lp"], 2 * i + n0 + n0 - NCH + 1)
                    e.tensor_scalar(oh, iot, sm[:, 0:1], None, ALU.is_equal).then_inc(S["s_lp"], 1)

                def hop_pool(e, i, n0, ms=s_msg[loops[0] - 1], src=vd[(k + 1) % 2 if k < 2 else 1]):
                    e.wait_ge(S["s_lp"], 2 * i + n0 + n0 - NCH + 1)
                    e.sem_inc(S["s_pl"], 1)
                    e.indirect_dma_start(msg, None, src[:, :],
                                         bass.IndirectOffsetOnAxis(ap=smi[:, 0:1], axis=0)).then_inc(ms, 16)

                def hop_pe(e, i, n0, ms=s_msg[loops[0] - 1], tiles=tiles, accs=accs):
                    e.wait_ge(S["s_lp"], 2 * i + n0 + n0 - NCH + 2)
                    e.wait_ge(ms, i * 16 + 16)
                    for n, t in enumerate(tiles):
                        mm = e.matmul(accs[t], oh[:, n * P:(n + 1) * P], msg, start=False, stop=False,
                                      skip_group_check=True)
                    mm.then_inc(S["s_ld"], 1)

                loop({"dve": hop_dve, "pool": hop_pool, "pe": hop_pe}, loops[0])
                for t in tiles:
                    acc = accs[t]
                    if k > 0:
                        v_out(t, acc, k % 2)
                        continue
                    if L < 2:
                        op("dve", lambda e, L=L, t=t: e.tensor_scalar(wt, bb[:, L, :], cst[:, 2, t:t + 1], None,
                                                                      ALU.mult))
                        op("dve", lambda e, acc=acc: e.tensor_tensor(wu, acc, wt, ALU.add))
                        op("dve", lambda e: e.tensor_scalar(gt, wu, 0.0, None, ALU.max))
                        turned(t)
                        continue
                    op("sp", lambda e, t=t: e.dma_start(xt[0:rows(t), :], x[t * P:t * P + rows(t), :]), 16)
                    op("dve", lambda e, t=t, acc=acc: e.scalar_tensor_tensor(wt, acc, cst[:, 3, t:t + 1],
                                                                             bb[:, 2, :], ALU.mult, ALU.add))
                    op("dve", lambda e: e.tensor_tensor(wu, wt, xt, ALU.add))
                    ln = lnb[:, 0, :]
                    op("dve", lambda e: e.bn_stats(ln[:, 0:6], wu))
                    op("dve", lambda e: e.bn_aggr(ln[:, 6:8], ln[:, 0:6]))
                    op("dve", lambda e: e.tensor_scalar(ln[:, 7:8], ln[:, 7:8], EPS, None, ALU.add))
                    op("act", lambda e: e.activation(ln[:, 8:9], ln[:, 7:8], ACT.Sqrt))
                    op("dve", lambda e: e.reciprocal(ln[:, 9:10], ln[:, 8:9]))
                    op("dve", lambda e: e.scalar_tensor_tensor(ln[:, 10:11], ln[:, 9:10], ln[:, 7:8], ln[:, 8:9],
                                                               ALU.mult, ALU.add))
                    op("dve", lambda e: e.reciprocal(ln[:, 11:12], ln[:, 10:11]))
                    op("dve", lambda e: e.tensor_scalar(ln[:, 9:10], ln[:, 11:12], 2.0, None, ALU.mult))
                    op("dve", lambda e: e.tensor_scalar(gt, wu, ln[:, 6:7], ln[:, 9:10], ALU.subtract, ALU.mult))
                    op("sp", lambda e, t=t: e.dma_start(out[t * P:t * P + rows(t), :], gt[0:rows(t), :]), 16)

    def run(eng, name):
        turn = 0
        for n, (who, fn, inc) in enumerate(line):
            if n == 0:
                if name == who:
                    fn(eng)
                turn = 1
                continue
            if who == "loop":
                if name in fn:
                    eng.wait_ge(S["s_turn"], turn)
                    with eng.Fori(0, NCH) as i:
                        fn[name](eng, i, inc * NCH)
                    if name == "pe":
                        eng.wait_ge(S["s_ld"], (inc + 1) * NCH + 1)
                        eng.sem_inc(S["s_turn"], 1)
                turn += 1
                continue
            if who == name:
                eng.wait_ge(S["s_turn"], turn)
                fn(eng).then_inc(S["s_turn"], inc)
            turn += inc
        eng.wait_ge(S["s_turn"], turn)

    return run


def groups_of(t):
    last = [-1] + [min(NG - 1, (P * (i + 1) - 1) // GW) for i in range(NT)]
    return list(range(last[t] + 1, last[t + 1] + 1)) if t < NT else []


def trailing(sched, empty, split):
    out = []
    held = None
    for it in sched:
        if it[0] == "T":
            out.append(it)
            continue
        L, k, t = it[1:]
        if k == 2 and held:
            out.append(held)
            held = None
        if (L, k) == (0, 2):
            gs = [("B", gi) for gi in groups_of(t + 1)]
            before = ("P", 0, 2, t - 1), ("V", 0, 2, t - 1)
            out += (gs[:empty] + ([before[0]] if t else []) + gs[empty:split] + ([before[1]] if t else [])
                    + gs[split:])
            if t == NT - 1:
                out += [it, ("V",) + it[1:]]
            continue
        out.append(it)
        if held:
            out.append(held)
        held = ("V",) + it[1:] if k > 0 else None
        if held and (L, k) != (0, 3):
            out.append(held)
            held = None
    return out


def bass_tag_gnn_layernorm(nc, x, table, heads, edges, Ws, bs, vd, degd, out):
    SCHED = schedule()
    pe_no, v_no, t_no = {}, {}, {}
    for it in SCHED:
        if it[0] == "T":
            t_no[it[1:]] = len(t_no)
        else:
            pe_no[it[1:]] = len(pe_no)
            if it[2] > 0:
                v_no[it[1:]] = len(v_no)
    p_of = {e: key for key, e in pe_no.items()}
    vbuf = {(L, k): (L + 3 - k) % 2 for L in range(3) for k in (3, 2, 1)}

    with ExitStack() as ctx:
        def sb(name, shape, dt):
            return ctx.enter_context(nc.sbuf_tensor(name, shape, dt))

        def ps(name, shape, dt):
            return ctx.enter_context(nc.psum_tensor(name, shape, dt))

        def sem(name):
            return ctx.enter_context(nc.semaphore(name))

        A8 = sb("A8", [P, NT, NP], F8)
        V = [sb(f"V{i}", [P, NT, 512], F16) for i in range(2)]
        AT = sb("AT", [P, NP], F16)
        gT = sb("gT", [P, NT, 2, 2, P], F16)
        Whl = sb("Whl", [P, 3, 2, 4, 512], F16)
        bb = sb("bb", [P, 3, F], F32)
        identf = sb("identf", [P, P], F32)
        stat = sb("stat", [P, 12 * NT + 3], F32)
        ast = sb("ast", [P, NAM], F32)
        ones16 = sb("ones16", [P, 2], F16)
        thS = sb("thS", [P, GD + 1], F32)
        cS = sb("cS", [P, len(AQ), GD + 1], F32)
        cD = sb("cD", [P, len(AQ), GD], F32)
        dgw = sb("dgw", [P, QW, GD], F32)
        dgT = sb("dgT", [NT, P], F32)
        thr = sb("thr", [P, 2, QW], F32)
        idx = sb("idx", [P, 8], I32)
        dg = sb("dg", [P, 8, NT], F32)
        cst = sb("cst", [P, 5, NT], F32)
        xr = sb("xr", [P, RB, F], F32)
        t1 = sb("t1", [P, RB, F], F32)
        w = sb("w", [P, RB, F], F32)
        g = sb("g", [P, RB, F], F32)
        lnb = sb("lnb", [P, RB, 12], F32)
        chk = sb("chk", [P, 40], F32)
        want = sb("want", [1, 4], F32)
        flag = sb("flag", [1, 2], I32)
        onesf = sb("onesf", [P, 2], F32)

        v1 = V[1][:, :, :].rearrange("p a b -> p (a b)")
        Wraw = v1[:, 0:4096].bitcast(F32).rearrange("p (m n) -> p m n", m=8)
        Wsc = v1[:, 4096:8192].bitcast(F32).rearrange("p (m n) -> p m n", m=8)
        w12 = Whl[:, 1:3, :, :, :].rearrange("p l c k n -> p (l c k n)")
        OB = w12[:, 0:NO * P * BV].rearrange("p (r j v) -> p r j v", r=NO, v=BV)
        OK = w12[:, 3072:3072 + NO * KEYS * BV].rearrange("p (r j v) -> p r j v", r=NO, v=BV)
        iotaB = w12[:, 5472:5472 + P * BV].rearrange("p (j v) -> p j v", v=BV)
        KKb = w12[:, 6496:6496 + NB * BV]
        KBb = w12[:, 7280:7280 + NB * BV]
        v0 = V[0][:, :, :].rearrange("p a b -> p (a b)")
        g1 = gT[:, :, :, :, :].rearrange("p a b c d -> p (a b c d)")
        LT = ([v0[:, i * JW:(i + 1) * JW] for i in range(14)] + [g1[:, i * JW:(i + 1) * JW] for i in range(10)]
              + [AT[:, 0:JW]])
        iotaJ = AT[:, JW:2 * JW]
        G = g1[:, 8960:8960 + 4 * JW].bitcast(I32).rearrange("p (q s e) -> p q s e", q=QW, s=2)
        wf, gf, tf = (z[:, :, :].rearrange("p a b -> p (a b)") for z in (w, g, t1))
        hI, hs, hb = tf[0:HP, 0:HN].bitcast(I32), tf[0:HP, 32:32 + HN], tf[0:HP, 64:64 + HN]

        bank = [ps(f"pb{i}", [P, 512], F32) for i in range(8)]
        bank_of, free, user = {}, [0, 1, 2, 5, 6], {}
        for e, (L, k, t) in p_of.items():
            if (L, k, t) == (0, 2, 0):
                bank_of[e] = 7
                continue
            few = (L, k) == (0, 2) or (L, k) == (0, 3) and t >= NT - 4
            b = next(i for i in free if not few or i < 5)
            free.remove(b)
            free.append(b)
            bank_of[e] = b
            before = [f for f in range(e) if bank_of[f] == b]
            if before:
                user[e] = before[-1]
        last_init = max(e for e in range(NT) if bank_of[e] > 4)
        PB = [bank[bank_of[e]] for e in range(len(p_of))]
        TB = bank[3:5]
        BB = bank[5:7]

        names = ("s_h s_w s_b s_cst s_cnt s_idx s_wk s_ki s_kt s_kb s_ka s_lt s_la s_hs s_vis s_ev "
                 "s_ob s_dw s_dr s_dt s_wq s_wi s_deg s_dg s_sq s_cs s_whi s_wp s_ps s_a1 s_d1 s_a2 "
                 "s_v s_gx s_g s_tp s_th s_tl s_z s_ln s_sd s_o s_dd s_st s_ck s_pk s_flag s_turn s_lp "
                 "s_ld s_pl s_at s_sg s_dl").split()
        S = {n: sem(n) for n in names}
        t2 = w[:, 2:4, :]
        s_xl = [sem(f"s_xl{i}") for i in range(RB)]
        s_ol = [sem(f"s_ol{i}") for i in range(RB)]
        s_msg = [sem(f"s_msg{i}") for i in range(9 * NQ)]
        s_gl = [sem(f"s_gl{i}") for i in range(NQ)]
        block = ctx.enter_context(nc.Block())
        general = general_path(nc, x, edges, Ws, bb, vd, out, A8, bank, cst, dg, w, g, lnb, identf, onesf, S, s_msg)

        def ending(eng, name):
            eng.wait_ge(S["s_flag"], 1)
            bad = eng.value_load(flag[0:1, 0:1], min_val=0, max_val=1)
            with eng.If(bad != 0):
                general(eng, name)


        @block.sync
        def _(sp):
            def store(t):
                sp.wait_ge(S["s_o"], t + 1)
                sp.dma_start(out[t * P:t * P + rows(t), :], g[0:rows(t), t % RB, :]).then_inc(s_ol[t % RB], 16)

            sp.dma_start(hI, heads.rearrange("(p i) -> p i", i=HN)).then_inc(S["s_h"], 16)
            for c in range(2):
                sp.dma_start(Wraw[:, 4 * c:4 * c + 4, :], Ws[0][:, c * P:(c + 1) * P, :].rearrange("k f n -> f k n"))\
                  .then_inc(S["s_w"], 16)
            for i in range(RB):
                sp.dma_start(xr[:, i, :], x[i * P:(i + 1) * P, :]).then_inc(s_xl[i], 16)
            for L in range(3):
                sp.dma_start(bb[:, L, :], bs[L].rearrange("(a n) -> a n", a=1).broadcast_to([P, F])).then_inc(S["s_b"], 16)
            sp.wait_ge(S["s_dw"], 2)
            sp.dma_start(degd.rearrange("(q p w) -> p q w", q=QW, w=GD), dgw[:, :, :]).then_inc(S["s_dr"], 16)
            sp.wait_ge(S["s_dr"], 16)
            sp.dma_start(dgT[:, :], degd[0:NP].rearrange("(a b) -> a b", b=P)).then_inc(S["s_dt"], 16)
            for i in range(RB, XL):
                if i < NT + RB:
                    sp.wait_ge(S["s_gx"], i - RB + 1)
                elif i < NT + 16 + RB:
                    sp.wait_ge(S["s_wq"], 3 * (i - RB - NT) + 3)
                else:
                    sp.wait_ge(S["s_z"], i - RB - NT - 16 + 1)
                if NT <= i < NT + 16:
                    L, c, k = 1 + (i - NT) // 8, (i - NT) // 4 % 2, (i - NT) % 4
                    sp.dma_start(xr[:, i % RB, :], Ws[L][k, c * P:(c + 1) * P, :]).then_inc(s_xl[i % RB], 16)
                    continue
                t = i if i < NT else i - NT - 16
                sp.dma_start(xr[0:rows(t), i % RB, :], x[t * P:t * P + rows(t), :]).then_inc(s_xl[i % RB], 16)
                if i - NT - 16 - RB >= 0:
                    store(i - NT - 16 - RB)
            for t in range(NT - RB, NT):
                store(t)
            for i in range(RB):
                sp.wait_ge(s_ol[i], 16 * len(range(i, NT, RB)))
            ending(sp, "sp")

        @block.gpsimd
        def _(pool):
            iota = dict(channel_multiplier=0, allow_small_or_imprecise_dtypes=True)
            pool.memset(ones16[:, 0:1], 1.0).then_inc(S["s_cst"], 1)
            pool.iota(iotaJ, pattern=[[1, JW]], base=0, **iota).then_inc(S["s_cst"], 1)
            pool.memset(ones16[:, 1:2], 0.5).then_inc(S["s_cst"], 1)
            pool.iota(thr[:, 0, :], pattern=[[GD * P, QW]], base=0, channel_multiplier=GD,
                      allow_small_or_imprecise_dtypes=True).then_inc(S["s_cst"], 1)
            pool.wait_ge(S["s_cst"], 4)
            pool.tensor_scalar(thr[:, 1, :], thr[:, 0, :], 1.5, 0.0, ALU.add, ALU.add).then_inc(S["s_cst"], 1)
            pool.iota(thS[:, :], pattern=[[-2, GD + 1]], base=GD, **iota).then_inc(S["s_cst"], 1)
            pool.memset(identf[:, :], 0.0).then_inc(S["s_cst"], 1)
            pool.wait_ge(S["s_cst"], 7)
            pool.affine_select(out=identf[:, :], in_=identf[:, :], compare_op=ALU.not_equal, fill=1.0, base=0,
                               pattern=[[-1, P]], channel_multiplier=1).then_inc(S["s_cst"], 1)
            pool.iota(iotaB, pattern=[[1, P], [0, BV]], base=0, **iota).then_inc(S["s_cst"], 1)
            pool.memset(want[:, 0:1], float(E)).then_inc(S["s_cst"], 1)
            pool.memset(want[:, 1:2], 0.0).then_inc(S["s_cst"], 1)
            pool.memset(want[:, 2:3], 15.0).then_inc(S["s_cst"], 1)
            pool.memset(onesf[:, :], 1.0).then_inc(S["s_cst"], 1)
            pool.memset(A8[:, :, (NG - 1) * GW:NP], 0.0).then_inc(S["s_cst"], 1)
            pool.wait_ge(S["s_idx"], 1)
            for c, (q0, q1) in enumerate(CHUNK):
                for q in range(q0, q1):
                    pool.indirect_dma_start(G[:, q, :, :].rearrange("p s e -> p (s e)"), None, table[:, :],
                                            bass.IndirectOffsetOnAxis(ap=idx[:, q:q + 1], axis=0)).then_inc(s_gl[c], 16)
            pool.wait_ge(S["s_w"], 32)
            hl = Whl[:, 0].rearrange("p c k n -> p (c k) n")
            pool.tensor_scalar(Wsc, Wraw, SV * SC, None, ALU.mult).then_inc(S["s_wp"], 1)
            pool.wait_ge(S["s_whi"], 1)
            pool.wait_ge(S["s_wp"], 1)
            pool.tensor_scalar(Wraw, hl[:, :, 0:F], SC, None, ALU.mult).then_inc(S["s_wp"], 1)
            pool.wait_ge(S["s_wp"], 2)
            pool.tensor_tensor(hl[:, :, F:512], Wsc, Wraw, ALU.subtract).then_inc(S["s_wp"], 1)
            pool.wait_ge(S["s_cs"], 1)
            for t in range(NT):
                pool.wait_ge(s_xl[t % RB], 16 * (t // RB + 1))
                if t >= RB:
                    pool.wait_ge(S["s_tp"], t - RB + 1)
                pool.tensor_scalar(g[:, t % RB, :], xr[:, t % RB, :], cst[:, 2, t:t + 1], 0.0, ALU.mult,
                                   ALU.add).then_inc(S["s_gx"], 1)
            for t in range(NT):
                pool.wait_ge(S["s_ev"], groups_of(t)[-1] + 1)
                src = A8[0:HALF, NT - 1, t * P:(t + 1) * P]
                pool.tensor_copy(AT[0:HALF, t * P:(t + 1) * P], src).then_inc(S["s_at"], 1)
                pool.wait_ge(S["s_at"], 2 * t + 1)
                pool.tensor_scalar(AT[HALF:P, t * P:(t + 1) * P], AT[0:HALF, t * P:(t + 1) * P], 1.0 / SC, 0.0, ALU.mult,
                                   ALU.add).then_inc(S["s_at"], 1)
            for i in range(16):
                L, c, k = 1 + i // 8, i // 4 % 2, i % 4
                raw = xr[:, (NT + i) % RB, :]
                pool.wait_ge(S["s_wi"], i + 1)
                pool.tensor_scalar(raw, raw, SV, 0.0, ALU.mult, ALU.add).then_inc(S["s_wq"], 1)
                pool.wait_ge(S["s_wq"], 3 * i + 1)
                pool.tensor_tensor(raw, raw, Whl[:, L, c, k, 0:F], ALU.subtract).then_inc(S["s_wq"], 1)
                pool.wait_ge(S["s_wq"], 3 * i + 2)
                pool.tensor_scalar(Whl[:, L, c, k, F:512], raw, SC, 0.0, ALU.mult, ALU.add).then_inc(S["s_wq"], 1)
            ending(pool, "pool")

        @block.scalar
        def _(act):
            act.wait_ge(S["s_cst"], 1)
            act.activation(lnb[:, 0, 0:1], ones16[:, 0:1], ACT.Sign)
            act.wait_ge(S["s_cst"], 2)
            act.wait_ge(S["s_hs"], 2)
            for i in AL:
                act.activation(LT[i][0:HP, :], iotaJ[0:HP, :], ACT.Sign, bias=hb[:, i:i + 1]).then_inc(S["s_la"], 1)
            act.wait_ge(S["s_w"], 32)
            act.activation(Whl[:, 0].rearrange("p c k n -> p (c k) n")[:, :, 0:F], Wraw, ACT.Copy,
                           scale=SV).then_inc(S["s_whi"], 1)
            act.wait_ge(S["s_cst"], CST)
            for c, (q0, q1) in enumerate(CHUNK):
                n0, n1 = q0 * P, min(q1 * P, NB * BV)
                act.wait_ge(S["s_dl"], c + 1)
                for q in [q for q in AQ if q0 <= q < q1]:
                    for i in range(GD + 1):
                        n = (q * (GD + 1) + i) * P
                        act.activation(v0[:, n:n + P], gf[:, q * P:(q + 1) * P], ACT.Sign, scale=2.0,
                                       bias=thS[:, i:i + 1], accum_out=cS[:, q, i:i + 1]).then_inc(S["s_sg"], 1)
                act.wait_ge(S["s_kt"], c + 1)
                act.activation(KBb[:, n0:n1], TB[1][:, 0:n1 - n0], ACT.Copy).then_inc(S["s_ka"], 1)
            act.activation(thS[:, 0:2], onesf[:, :], ACT.Sqrt)

            def columns(gi):
                n = min(GS, NW - gi * GS)
                act.wait_ge(S["s_vis"], gi + 1)
                act.activation(A8[:, :, gi * GW:gi * GW + n * GD].rearrange("p a (g w) -> p a g w", w=GD),
                               BB[gi % 2][:, 0:n * KEYS].rearrange("p (g a w) -> p a g w", a=NT, w=GD),
                               ACT.Copy, saturate=False).then_inc(S["s_ev"], 1)

            for gi in groups_of(0):
                columns(gi)
            act.wait_ge(S["s_dg"], 2)
            act.activation(dg[:, 2, :], dg[:, 1, :], ACT.Sqrt).then_inc(S["s_sq"], 1)
            act.wait_ge(S["s_cs"], 1)
            for it in trailing(SCHED, 0, 2):
                if it[0] == "B":
                    columns(it[1])
                    continue
                if it[0] == "T":
                    _, L, t = it
                    j = t_no[(L, t)]
                    act.wait_ge(S["s_tp"], j + 1)
                    act.activation(gT[:, t, :, 0, :], TB[j % 2][:, 0:F].rearrange("p (c m) -> p c m", c=2),
                                   ACT.Copy, scale=1.0 / SC).then_inc(S["s_th"], 1)
                    continue
                what, L, k, t = it
                e = pe_no[(L, k, t)]
                if what == "V":
                    v = v_no[(L, k, t)]
                    act.wait_ge(S["s_d1"], e + 1)
                    r = P if t < NT - 1 else HALF
                    act.activation(V[vbuf[(L, k)]][0:r, t, 0:F], PB[e][0:r, 0:F], ACT.Copy,
                                   scale=1.0 / SC).then_inc(S["s_a2"], 1)
                    if (L, k) == (0, 1) and t < 16:
                        i = NT + t
                        act.wait_ge(s_xl[i % RB], 16 * (i // RB + 1))
                        act.wait_ge(S["s_vis"], NG)
                        act.activation(Whl[:, 1 + t // 8, t // 4 % 2, t % 4, 0:F], xr[:, i % RB, :], ACT.Copy,
                                       scale=SV).then_inc(S["s_wi"], 1)
                    continue
                act.wait_ge(S["s_ps"], e + 1)
                if e >= RB:
                    act.wait_ge(S["s_d1"], e - RB + 1)
                lo = PB[e][:, F:512]
                if k > 0:
                    sc = cst[:, 0, t:t + 1]
                elif L < 2:
                    sc = 1.0 / SV
                else:
                    sc = cst[:, 4, t:t + 1]
                act.activation(t1[:, e % RB, :], lo, ACT.Copy, scale=sc).then_inc(S["s_a1"], 1)
                if k == 0 and L == 2:
                    act.wait_ge(S["s_ln"], t + 1)
                    act.activation(lnb[:, t % RB, 8:9], lnb[:, t % RB, 7:8], ACT.Sqrt).then_inc(S["s_sd"], 1)
            ending(act, "act")

        @block.tensor
        def _(pe):
            pe.wait_ge(S["s_cst"], 3)

            def emptied(was):
                if was[1] > 0:
                    pe.wait_ge(S["s_v"], v_no[was] + 1)
                else:
                    pe.wait_ge(S["s_d1"], pe_no[was] + 1)

            def build(gi):
                if gi == len(groups_of(0)):
                    emptied(p_of[last_init])
                if gi >= 2:
                    pe.wait_ge(S["s_ev"], gi - 1)
                for k in range(min(GS, NW - gi * GS)):
                    vis = GS * gi + k
                    b = vis // BV
                    if k == 0 or vis % BV == 0:
                        pe.wait_ge(S["s_ob"], 2 * b + 2)
                    mm = pe.matmul(BB[gi % 2][:, k * KEYS:(k + 1) * KEYS], OB[:, b % NO, :, vis % BV],
                                   OK[:, b % NO, :, vis % BV], start=(k == 0), stop=True, skip_group_check=True)
                mm.then_inc(S["s_vis"], 1)

            for i in range(HN):
                on_act = sum(a <= i for a in AL)
                if i in AL:
                    pe.wait_ge(S["s_la"], on_act)
                else:
                    pe.wait_ge(S["s_lt"], i + 1 - on_act)
                for q in range(QW):
                    mm = pe.matmul(bank[7][:, q:q + 1], LT[i][0:HP, q * P:(q + 1) * P], ones16[0:HP, int(i in AL):int(i in AL) + 1],
                                   start=(i == 0 and q == 0), stop=(i == HN - 1), skip_group_check=True)
            mm.then_inc(S["s_cnt"], 1)
            pe.wait_ge(S["s_cst"], CST)
            for c, (q0, q1) in enumerate(CHUNK):
                pe.wait_ge(S["s_ki"], c + 1)
                pe.wait_ge(S["s_kb"], c)
                pe.wait_ge(S["s_ka"], c)
                for m in range(2):
                    for q in range(q1 - q0):
                        src = tf[:, 384 * m + q * P:384 * m + (q + 1) * P]
                        mm = pe.transpose(TB[m][:, q * P:(q + 1) * P], src, identf[:, :])
                mm.then_inc(S["s_kt"], 1)
            for gi in groups_of(0):
                build(gi)
            pe.wait_ge(S["s_dt"], 16)
            pe.transpose(bank[7][:, 0:NT], dgT[:, :], identf[0:NT, 0:NT]).then_inc(S["s_deg"], 1)
            pe.wait_ge(S["s_wp"], 3)
            def work(it, within={}):
                if it[0] == "T":
                    _, L, t = it
                    j = t_no[(L, t)]
                    if L == 0:
                        pe.wait_ge(S["s_gx"], t + 1)
                    else:
                        pe.wait_ge(S["s_g"], j - NT + 1)
                    if j >= 2:
                        pe.wait_ge(S["s_tl"], j - 1)
                    for c in range(2):
                        mm = pe.transpose(TB[j % 2][:, c * P:(c + 1) * P], g[:, j % RB, c * P:(c + 1) * P],
                                          identf[:, :])
                    mm.then_inc(S["s_tp"], 1)
                    return
                _, L, k, t = it
                e = pe_no[(L, k, t)]
                if e in user:
                    emptied(p_of[user[e]])
                elif bank_of[e] > 4:
                    pe.wait_ge(S["s_ev"], len(groups_of(0)))
                if (L, k, t) == (0, 1, 0):
                    pe.wait_ge(S["s_ev"], NG)
                if (L, k, t) == (1, 3, 0):
                    pe.wait_ge(S["s_wq"], 48)
                if k == 3:
                    pe.wait_ge(S["s_tl"], t_no[(L, t)] + 1)
                acc = PB[e]
                for c in range(2):
                    pe.matmul(acc[:, :], gT[:, t, c, 0, :], Whl[:, L, c, k, :], start=(c == 0), stop=False,
                              skip_group_check=True)
                    mm = pe.matmul(acc[:, F:512], gT[:, t, c, 1, :], Whl[:, L, c, k, 0:F], start=False,
                                   stop=(k == 3 and c == 1), skip_group_check=True)
                if k < 3:
                    src = V[vbuf[(L, k + 1)]]
                    coming = groups_of(t + 1) if (L, k) == (0, 2) else []
                    if (L, k) == (0, 2):
                        pe.wait_ge(S["s_ev"], groups_of(t)[-1] + 1)
                    for a in range(NT):
                        for other in within.get(a, ()):
                            work(other)
                        if (L, k, t) == (0, 2, 0):
                            for gi in coming[2 * (a - NT + 4):2 * (a - NT + 4) + 2] if a >= NT - 4 else ():
                                build(gi)
                        elif a % 3 == 0 and a // 3 < len(coming):
                            build(coming[a // 3])
                        if t == 0:
                            pe.wait_ge(S["s_v"], v_no[(L, k + 1, a)] + 1)
                        if a < NT - 1:
                            mm = pe.matmul(acc[:, :], A8[:, a, t * P:(t + 1) * P], src[:, a, :], start=False,
                                           stop=False, skip_group_check=True)
                            continue
                        if (L, k) == (0, 2):
                            pe.wait_ge(S["s_at"], 2 * t + 2)
                        mm = pe.matmul(acc[:, 0:F], AT[:, t * P:(t + 1) * P], src[:, a, 0:F], start=False,
                                       stop=True, skip_group_check=True)
                mm.then_inc(S["s_ps"], 1)
                if (L, k, t) == (2, 0, 13):
                    pe.wait_ge(S["s_ck"], 1)
                    pe.transpose(bank[7][0:15, 0:P], chk[:, 0:15], identf[:, :]).then_inc(S["s_pk"], 1)
                if (L, k, t) == (2, 0, 18):
                    pe.wait_ge(S["s_ck"], 2)
                    pe.matmul(bank[7][0:1, 128:130], onesf[:, 0:1], chk[:, 15:17], start=True, stop=True)
                    pe.matmul(bank[7][0:1, 130:131], onesf[0:15, 0:1], chk[0:15, 21:22], start=True,
                              stop=True).then_inc(S["s_pk"], 1)
            within = {}
            for it in SCHED:
                k, t = (3, it[2]) if it[0] == "T" else it[2:]
                if k == 3 and it[1] == 0 and t >= AHEAD + 2 * (it[0] == "T"):
                    within.setdefault(t - AHEAD - 2 * (it[0] == "T"), []).append(it)
                elif it[1] > 0 and (t == NT - 1 and k == 3 or k == 3 and t == NT - 2 and it[0] == "P"):
                    within.setdefault(WT if it[0] == "T" else WP if t == NT - 1 else WQ, []).append(it)
                elif (k, t) == (2, 0):
                    work(it, within)
                    within = {}
                else:
                    work(it)
            ending(pe, "pe")

        @block.vector
        def _(dve):
            dve.wait_ge(S["s_h"], 16)
            dve.tensor_scalar(hs, hI, 1.0 / GD, None, ALU.mult).then_inc(S["s_hs"], 1)
            dve.wait_ge(S["s_hs"], 1)
            dve.wait_ge(S["s_cst"], 2)
            dve.tensor_scalar(hb, hs, -1.0, -0.125, ALU.mult, ALU.add).then_inc(S["s_hs"], 1)
            for i in range(HN):
                if i in AL:
                    continue
                dve.tensor_scalar(LT[i][0:HP, :], iotaJ[0:HP, :], hs[:, i:i + 1], None, ALU.is_gt).then_inc(S["s_lt"], 1)
            dve.wait_ge(S["s_cnt"], 1)
            dve.tensor_scalar(idx[:, 0:QW], bank[7][:, 0:QW], 0.5 * HP * len(AL) - 1.0, 0.0, ALU.add, ALU.max).then_inc(S["s_idx"], 1)
            kk = 0

            def link(ins):
                nonlocal kk
                kk += 1
                ins.then_inc(S["s_wk"], 1)
                dve.wait_ge(S["s_wk"], kk)

            dve.wait_ge(S["s_cst"], CST)
            junk = 0
            for c, (q0, q1) in enumerate(CHUNK):
                dve.wait_ge(s_gl[c], 16 * (q1 - q0))
                n = q1 - q0

                def part(ap, at):
                    return ap[:, at:at + n * P].rearrange("p (q e) -> p q e", q=n)

                s_, d_ = G[:, q0:q1, 0, :], G[:, q0:q1, 1, :]
                ai, bi = part(wf.bitcast(I32), 0), part(wf.bitcast(I32), 384)
                kf, sq, dl = part(wf, 0), part(wf, 384), part(gf, q0 * P)
                link(dve.tensor_tensor(dl, d_, thr[:, 1, q0:q1].unsqueeze(2).broadcast_to([P, n, P]), ALU.subtract))
                dve.sem_inc(S["s_dl"], 1)
                for q in [q for q in range(q0, q1) if q not in AQ]:
                    for i in range(GD):
                        last = dve.tensor_scalar(v0[:, 3072 + junk * P:3072 + (junk + 1) * P], gf[:, q * P:(q + 1) * P],
                                                 i - 1.5, None, ALU.is_equal, ALU.add, accum_out=dgw[:, q, i:i + 1])
                        junk += 1
                if c == 2:
                    last.then_inc(S["s_dw"], 1)
                    dve.wait_ge(S["s_sg"], len(AQ) * (GD + 1))
                    link(dve.tensor_tensor(cD[:, :, :], cS[:, :, 0:GD], cS[:, :, 1:GD + 1], ALU.subtract))
                    dve.tensor_scalar(dgw[:, 0:len(AQ), :], cD[:, :, :], 0.5, None, ALU.mult).then_inc(S["s_dw"], 1)
                link(dve.tensor_scalar(bi, s_, P - 1, None, ALU.bitwise_and))
                link(dve.tensor_scalar(ai, s_, 7, None, ALU.logical_shift_right))
                if c:
                    dve.wait_ge(S["s_kt"], c)
                link(dve.tensor_copy(part(tf, 384), bi))
                link(dve.tensor_tensor(sq, dl, dl, ALU.mult))
                link(dve.scalar_tensor_tensor(kf, ai, float(GD), dl, ALU.mult, ALU.add))
                link(dve.tensor_scalar(sq, sq, 2.5, FAR, ALU.is_gt, ALU.mult))
                dve.tensor_tensor(part(tf, 0), kf, sq, ALU.add).then_inc(S["s_ki"], 1)
                n0, n1 = q0 * P, min(q1 * P, NB * BV)
                dve.wait_ge(S["s_kt"], c + 1)
                dve.tensor_scalar(KKb[:, n0:n1], TB[0][:, 0:n1 - n0], 1.5, None, ALU.add).then_inc(S["s_kb"], 1)

            nb = 0

            def onehots(gi):
                nonlocal nb
                while nb < NB and BV * nb <= GS * (gi + 1) - 1:
                    if nb == 0:
                        dve.wait_ge(S["s_kb"], len(CHUNK))
                        dve.wait_ge(S["s_ka"], len(CHUNK))
                    if nb >= NO:
                        dve.wait_ge(S["s_vis"], (BV * (nb - NO) + BV - 1) // GS + 1)
                    at = slice(BV * nb, BV * (nb + 1))
                    dve.tensor_tensor(OB[:, nb % NO, :, :], iotaB, KBb[:, at].unsqueeze(1).broadcast_to([P, P, BV]),
                                      ALU.is_equal).then_inc(S["s_ob"], 1)
                    dve.tensor_tensor(OK[:, nb % NO, :, :], iotaB[:, 0:KEYS, :],
                                      KKb[:, at].unsqueeze(1).broadcast_to([P, KEYS, BV]),
                                      ALU.is_equal).then_inc(S["s_ob"], 1)
                    nb += 1

            for gi in groups_of(0):
                onehots(gi)
            nd = 0

            def dl_(ins):
                nonlocal nd
                nd += 1
                ins.then_inc(S["s_dd"], 1)
                dve.wait_ge(S["s_dd"], nd)

            dve.wait_ge(S["s_deg"], 1)
            dve.tensor_copy(dg[:, 0, :], bank[7][:, 0:NT]).then_inc(S["s_dg"], 1)
            dve.wait_ge(S["s_dg"], 1)
            dve.tensor_scalar(dg[:, 1, :], dg[:, 0, :], 1.0, None, ALU.max).then_inc(S["s_dg"], 1)
            dve.wait_ge(S["s_dg"], 2)
            dl_(dve.reciprocal(dg[:, 3, :], dg[:, 1, :]))
            dl_(dve.tensor_scalar(dg[:, 4, :], dg[:, 0, :], 1.0, None, ALU.min))
            dl_(dve.tensor_tensor(cst[:, 0, :], dg[:, 3, :], dg[:, 4, :], ALU.mult))
            dl_(dve.tensor_scalar(cst[:, 1, :], cst[:, 0, :], SC, None, ALU.mult))
            dve.wait_ge(S["s_sq"], 1)
            dl_(dve.reciprocal(dg[:, 5, :], dg[:, 2, :]))
            dl_(dve.tensor_tensor(dg[:, 6, :], dg[:, 5, :], dg[:, 1, :], ALU.mult))
            dl_(dve.tensor_tensor(dg[:, 7, :], dg[:, 6, :], dg[:, 2, :], ALU.add))
            dl_(dve.tensor_scalar(cst[:, 2, :], dg[:, 7, :], 0.5 * SC, None, ALU.mult))
            dl_(dve.reciprocal(dg[:, 5, :], dg[:, 7, :]))
            dl_(dve.tensor_scalar(cst[:, 3, :], dg[:, 5, :], 2.0 / SV, None, ALU.mult))
            dve.tensor_scalar(cst[:, 4, :], dg[:, 5, :], 2.0 / (SV * SC), None, ALU.mult).then_inc(S["s_cs"], 1)
            onehots(len(groups_of(0)) + 2)
            dve.wait_ge(S["s_cs"], 1)
            dve.wait_ge(S["s_b"], 48)
            nst = nam = 0

            def largest(col, ap, axis):
                nonlocal nst
                dve.tensor_reduce(stat[:, col:col + 1], ap, axis, ALU.max,
                                  apply_absolute_value=True).then_inc(S["s_st"], 1)
                nst += 1

            def verdict(part):
                if part == 0:
                    verdict_maxima()
                elif part == 1:
                    verdict_ranges()
                else:
                    dve.wait_ge(S["s_pk"], 2)
                    dl_(dve.tensor_copy(chk[0:1, 24:27], bank[7][0:1, 128:131]))
                    dl_(dve.tensor_tensor(chk[0:1, 28:31], chk[0:1, 24:27], want[:, 0:3], ALU.not_equal))
                    dve.tensor_reduce(flag[:, 0:1], chk[0:1, 28:31], AX.X, ALU.max).then_inc(S["s_flag"], 1)

            def verdict_maxima():
                assert nam == NAM
                dve.wait_ge(S["s_st"], nst)
                dl_(dve.tensor_reduce(chk[:, 0:12], stat[:, 0:12 * NT].rearrange("p (m t) -> p m t", t=NT), AX.X,
                                      ALU.max))
                dl_(dve.tensor_copy(chk[:, 12:15], stat[:, 12 * NT:12 * NT + 3]))
                dl_(dve.tensor_reduce(chk[:, 15:16], dg[:, 0, :], AX.X, ALU.add))
                dl_(dve.tensor_reduce(chk[:, 17:18], ast[:, :], AX.X, ALU.max))
                dve.tensor_scalar(chk[:, 16:17], chk[:, 17:18], AMAX, None, ALU.is_ge).then_inc(S["s_ck"], 1)

            def verdict_ranges():
                dve.wait_ge(S["s_pk"], 1)
                dl_(dve.tensor_reduce(chk[0:15, 18:19], bank[7][0:15, 0:P], AX.X, ALU.max))
                dl_(dve.tensor_scalar(chk[0:15, 19:20], chk[0:15, 18:19], LOW, None, ALU.is_ge))
                dl_(dve.tensor_scalar(chk[0:15, 20:21], chk[0:15, 18:19], HIGH, None, ALU.is_le))
                dve.tensor_tensor(chk[0:15, 21:22], chk[0:15, 19:20], chk[0:15, 20:21],
                                  ALU.mult).then_inc(S["s_ck"], 1)

            for it in trailing(SCHED, 4, 6):
                if it[0] == "B":
                    onehots(it[1])
                    continue
                if it[0] == "T":
                    _, L, t = it
                    j = t_no[(L, t)]
                    dve.wait_ge(S["s_th"], j + 1)
                    dve.scalar_tensor_tensor(gT[:, t, :, 1, :], gT[:, t, :, 0, :], -SC,
                                             TB[j % 2][:, 0:F].rearrange("p (c m) -> p c m", c=2),
                                             ALU.mult, ALU.add).then_inc(S["s_tl"], 1)
                    if L:
                        largest(9 * NT + j, gT[:, t, :, 0, :], AX.XY)
                    continue
                what, L, k, t = it
                e = pe_no[(L, k, t)]
                hi = PB[e][:, 0:F]
                we = w[:, t % 2, :]
                if k > 0:
                    v = v_no[(L, k, t)]
                    vb = V[vbuf[(L, k)]]
                if what == "V":
                    dve.wait_ge(S["s_a2"], v + 1)
                    if t < NT - 1:
                        lo, r = vb[:, t, F:512], P
                    else:
                        lo, r = vb[HALF:P, t, 0:F], HALF
                    dve.scalar_tensor_tensor(lo, vb[0:r, t, 0:F], -SC, hi[0:r, :], ALU.mult,
                                             ALU.add).then_inc(S["s_v"], 1)
                    if (L, k) not in ((0, 3), (0, 2)):
                        if t == NT - 1:
                            dve.wait_ge(S["s_v"], v + 1)
                        largest(v, vb[:, t, 0:F], AX.X)
                    if (L, k) == (0, 1):
                        largest(9 * NT + t, gT[:, t, :, 0, :], AX.XY)
                        largest(v_no[(0, 2, t)], V[vbuf[(0, 2)]][:, t, 0:F], AX.X)
                    if (L, k) == (1, 1) and t < 3:
                        largest(12 * NT + t, Whl[:, t].rearrange("p c k n -> p (c k) n")[:, :, 0:F], AX.XY)
                    if k < 3 and L > 0 and nam < NAM:
                        a_, i_ = nam // 4, nam % 4
                        dve.tensor_reduce(ast[:, nam:nam + 1], A8[:, a_, 800 * i_:800 * i_ + 800].bitcast(U8), AX.X,
                                          ALU.max).then_inc(S["s_st"], 1)
                        nam += 1
                        nst += 1
                    continue
                if k > 0:
                    if (L, k) == (0, 1):
                        largest(v_no[(0, 3, t)], vb[:, t, 0:F], AX.X)
                    dve.wait_ge(S["s_a1"], e + 1)
                    dve.scalar_tensor_tensor(hi, hi, cst[:, 1, t:t + 1], t1[:, e % RB, :], ALU.mult,
                                             ALU.add).then_inc(S["s_d1"], 1)
                elif L < 2:
                    j = t_no[(L + 1, t)]
                    dve.wait_ge(S["s_a1"], e + 1)
                    dl_(dve.scalar_tensor_tensor(t2[:, t % 2, :], bb[:, L, :], cst[:, 2, t:t + 1],
                                                 t1[:, e % RB, :], ALU.mult, ALU.add))
                    dve.scalar_tensor_tensor(we, hi, SC / SV, t2[:, t % 2, :], ALU.mult,
                                             ALU.add).then_inc(S["s_d1"], 1)
                    dve.wait_ge(S["s_d1"], e + 1)
                    dve.wait_ge(S["s_tp"], j - RB + 1)
                    dve.tensor_scalar(g[:, j % RB, :], we, 0.0, None, ALU.max).then_inc(S["s_g"], 1)
                else:
                    i = NT + 16 + t
                    if t in (10, 15, 20):
                        verdict((t - 10) // 5)
                    dve.wait_ge(s_xl[i % RB], 16 * (i // RB + 1))
                    r = rows(t)
                    dve.tensor_tensor(t2[:, t % 2, :], xr[:, i % RB, :], bb[:, 2, :], ALU.add).then_inc(S["s_z"], 1)
                    dve.wait_ge(S["s_a1"], e + 1)
                    dve.scalar_tensor_tensor(we, hi, cst[:, 3, t:t + 1], t1[:, e % RB, :], ALU.mult,
                                             ALU.add).then_inc(S["s_d1"], 1)
                    dve.wait_ge(S["s_d1"], e + 1)
                    dve.wait_ge(S["s_z"], t + 1)
                    dl_(dve.tensor_tensor(we, we, t2[:, t % 2, :], ALU.add))
                    ln = lnb[:, t % RB, :]
                    dl_(dve.bn_stats(ln[:, 0:6], we))
                    dl_(dve.bn_aggr(ln[:, 6:8], ln[:, 0:6]))
                    dve.tensor_scalar(ln[:, 7:8], ln[:, 7:8], EPS, None, ALU.add).then_inc(S["s_ln"], 1)
                    dve.wait_ge(S["s_sd"], t + 1)
                    dl_(dve.reciprocal(ln[:, 9:10], ln[:, 8:9]))
                    dl_(dve.scalar_tensor_tensor(ln[:, 10:11], ln[:, 9:10], ln[:, 7:8], ln[:, 8:9], ALU.mult, ALU.add))
                    dl_(dve.reciprocal(ln[:, 11:12], ln[:, 10:11]))
                    dl_(dve.tensor_scalar(ln[:, 9:10], ln[:, 11:12], 2.0, None, ALU.mult))
                    if t >= RB:
                        dve.wait_ge(s_ol[t % RB], 16 * (t // RB))
                    dve.tensor_scalar(g[:, t % RB, :], we, ln[:, 6:7], ln[:, 9:10], ALU.subtract,
                                      ALU.mult).then_inc(S["s_o"], 1)
            ending(dve, "dve")


def kernel(**inputs):
    import numpy as _np
    import concourse.bacc as _bacc
    from concourse import mybir as _mybir
    from concourse.bass_utils import run_bass_kernel_spmd as _run

    nc = _bacc.Bacc("TRN2", target_bir_lowering=False, num_devices=1)
    src = _np.asarray(inputs["src"])
    dst = _np.asarray(inputs["dst"])
    pad = _np.full(WIN, -1, _np.int32)
    srcp = _np.concatenate([src, _np.zeros(WIN, _np.int32)])
    dstp = _np.concatenate([dst, pad])
    at = _np.arange(0, E, GRAN)[:, None] + _np.arange(WIN)[None, :]
    arrays = {"x": _np.ascontiguousarray(inputs["x"]),
              "table": _np.ascontiguousarray(_np.concatenate([srcp[at], dstp[at]], axis=1)),
              "edges": _np.ascontiguousarray(_np.stack([_np.concatenate([src, _np.zeros(NCH * P - E, _np.int32)]),
                                                        dstp[:NCH * P]]).reshape(2, P, NCH)),
              "heads": _np.ascontiguousarray(dst[::GRAN])}
    for i in (1, 2, 3):
        arrays[f"W{i}"] = _np.ascontiguousarray(inputs[f"L0_gnn_W{i}"])
        arrays[f"b{i}"] = _np.ascontiguousarray(inputs[f"L0_gnn_b{i}"])
    ap = {k: nc.dram_tensor("in_" + k, v.shape, _mybir.dt.from_np(v.dtype), kind="ExternalInput").ap()
          for k, v in arrays.items()}
    out = nc.dram_tensor("out_0", (N, F), _mybir.dt.float32, kind="ExternalOutput").ap()
    degd = nc.dram_tensor("degd", (JW * GD,), _mybir.dt.float32, kind="Internal").ap()
    vd = [nc.dram_tensor(f"vd{i}", (NP, F), _mybir.dt.float32, kind="Internal").ap() for i in range(2)]
    bass_tag_gnn_layernorm(nc, ap["x"], ap["table"], ap["heads"], ap["edges"], [ap["W1"], ap["W2"], ap["W3"]],
                           [ap["b1"], ap["b2"], ap["b3"]], vd, degd, out)
    r = _run(nc, [{"in_" + k: v for k, v in arrays.items()}], core_ids=[0])
    return r.results[0]["out_0"]
```
